# Optimizing a Trainium2 kernel written in Bass

```python
import numpy as np
import jax
import jax.numpy as jnp

def _softmax(x, axis=-1):
    return jax.nn.softmax(x, axis=axis)

def _gelu(x):
    return jax.nn.gelu(x, approximate=True)

def _silu(x):
    return jax.nn.silu(x)

def _sigmoid(x):
    return jax.nn.sigmoid(x)

def _layernorm(x, axis=-1, eps=1e-05):
    m = jnp.mean(x, axis=axis, keepdims=True)
    v = jnp.var(x, axis=axis, keepdims=True)
    return (x - m) / jnp.sqrt(v + eps)

def _scatter_add(tgt, idx, src, axis=0):
    return tgt.at[idx].add(src)

def _segment_sum(src, seg, n):
    return jax.ops.segment_sum(src, seg, n)
kernel_name = 'mk_lm_tower_d1_tok_ids256_r4_a9478b'

def setup_inputs(seed: int=0):
    np.random.seed(seed)
    _w = jnp.asarray

    def _rec_inputs():
        import jax
        import jax.numpy as jnp
        _rk = jax.random.key(seed)
        x = jax.random.randint(jax.random.fold_in(_rk, 1), (128, 128), 0, 100001, jnp.int32)
        return x
    x = _rec_inputs()

    def _L0_tok_setup():
        import jax, jax.numpy as jnp
        import numpy as np
        NUM_ITEMS = 25000
        D = 64
        FOURIER_DIM = 64
        VISIT_DIM = 24
        RESIDUAL_SCALE = 0.1
        LN_EPS = 1e-05

        def _layer_norm(x, gamma, beta):
            mu = jnp.mean(x, axis=-1, keepdims=True)
            var = jnp.mean(jnp.square(x - mu), axis=-1, keepdims=True)
            return (x - mu) * jax.lax.rsqrt(var + LN_EPS) * gamma + beta
        key = jax.random.key(seed)
        ks = jax.random.split(key, 12)
        item_ids = jax.random.randint(ks[0], (128, 512), 0, NUM_ITEMS + 1)
        emb_table = 0.02 * jax.random.normal(ks[1], (NUM_ITEMS + 1, D), dtype=jnp.float32)
        emb_table = emb_table.at[0].set(0.0)
        geo_table = jax.random.normal(ks[2], (NUM_ITEMS + 1, FOURIER_DIM), dtype=jnp.float32)
        visit_table = jax.random.uniform(ks[3], (NUM_ITEMS + 1, VISIT_DIM), dtype=jnp.float32)

        def xavier(k, fan_in, fan_out):
            lim = np.sqrt(6.0 / (fan_in + fan_out))
            return jax.random.uniform(k, (fan_in, fan_out), jnp.float32, -lim, lim)
        w_item = xavier(ks[4], D, D)
        b_item = jnp.zeros((D,), jnp.float32)
        w_geo = xavier(ks[5], FOURIER_DIM, D)
        b_geo = jnp.zeros((D,), jnp.float32)
        w_visit = xavier(ks[6], VISIT_DIM, D)
        b_visit = jnp.zeros((D,), jnp.float32)
        w_fuse = xavier(ks[7], 3 * D, D)
        b_fuse = jnp.zeros((D,), jnp.float32)
        ln_gamma = jnp.ones((D,), jnp.float32)
        ln_beta = jnp.zeros((D,), jnp.float32)
        return dict(item_ids=item_ids, emb_table=emb_table, geo_table=geo_table, visit_table=visit_table, w_item=w_item, b_item=b_item, w_geo=w_geo, b_geo=b_geo, w_visit=w_visit, b_visit=b_visit, w_fuse=w_fuse, b_fuse=b_fuse, ln_gamma=ln_gamma, ln_beta=ln_beta)
    _L0_tok_all = _L0_tok_setup()
    _L0_tok_in = {k: v for k, v in _L0_tok_all.items() if k in ('emb_table', 'geo_table', 'visit_table', 'w_item', 'b_item', 'w_geo', 'b_geo', 'w_visit', 'b_visit', 'w_fuse', 'b_fuse', 'ln_gamma', 'ln_beta')}
    del _L0_tok_all

    def _L0_attn_setup():
        import jax, jax.numpy as jnp
        import numpy as np
        DIM = 64
        HEADS = 4
        HEAD_DIM = DIM // HEADS
        SCALE = HEAD_DIM ** (-0.5)
        key = jax.random.key(seed)
        ks = jax.random.split(key, 9)
        B, N, C = (2, 1024, DIM)
        x = jax.random.normal(ks[0], (B, N, C), dtype=jnp.float32)
        lim = np.sqrt(6.0 / (C + C)).astype(np.float32)

        def w(k):
            return jax.random.uniform(k, (C, C), dtype=jnp.float32, minval=-lim, maxval=lim)
        return {'x': x, 'Wq': w(ks[1]), 'bq': jnp.zeros((C,), jnp.float32), 'Wk': w(ks[2]), 'bk': jnp.zeros((C,), jnp.float32), 'Wv': w(ks[3]), 'bv': jnp.zeros((C,), jnp.float32), 'Wo': w(ks[4]), 'bo': jnp.zeros((C,), jnp.float32)}
    _L0_attn_all = _L0_attn_setup()
    _L0_attn_in = {k: v for k, v in _L0_attn_all.items() if k in ('Wq', 'bq', 'Wk', 'bk', 'Wv', 'bv', 'Wo', 'bo')}
    del _L0_attn_all

    def _L0_ffn_setup():
        import jax, jax.numpy as jnp
        import numpy as np
        B, S, D = (8, 1024, 64)
        H = 4 * D
        CAPACITY = 0.5
        key = jax.random.key(seed)
        ks = jax.random.split(key, 6)
        x = jax.random.normal(ks[0], (B, S, D), dtype=jnp.float32)
        attention_mask = jnp.zeros((B, 1, 1, S), dtype=jnp.float32)
        wr = jax.random.normal(ks[1], (D, 1), dtype=jnp.float32) * 0.02
        br = jnp.zeros((1,), dtype=jnp.float32)
        w1 = jax.random.normal(ks[2], (D, H), dtype=jnp.float32) * 0.02
        b1 = jnp.zeros((H,), dtype=jnp.float32)
        w2 = jax.random.normal(ks[3], (H, D), dtype=jnp.float32) * 0.02
        b2 = jnp.zeros((D,), dtype=jnp.float32)
        return {'x': x, 'attention_mask': attention_mask, 'wr': wr, 'br': br, 'w1': w1, 'b1': b1, 'w2': w2, 'b2': b2}
    _L0_ffn_all = _L0_ffn_setup()
    _L0_ffn_in = {k: v for k, v in _L0_ffn_all.items() if k in ('attention_mask', 'wr', 'br', 'w1', 'b1', 'w2', 'b2')}
    del _L0_ffn_all
    return {'x': x, 'L0_tok_emb_table': _L0_tok_in['emb_table'], 'L0_tok_geo_table': _L0_tok_in['geo_table'], 'L0_tok_visit_table': _L0_tok_in['visit_table'], 'L0_tok_w_item': _L0_tok_in['w_item'], 'L0_tok_b_item': _L0_tok_in['b_item'], 'L0_tok_w_geo': _L0_tok_in['w_geo'], 'L0_tok_b_geo': _L0_tok_in['b_geo'], 'L0_tok_w_visit': _L0_tok_in['w_visit'], 'L0_tok_b_visit': _L0_tok_in['b_visit'], 'L0_tok_w_fuse': _L0_tok_in['w_fuse'], 'L0_tok_b_fuse': _L0_tok_in['b_fuse'], 'L0_tok_ln_gamma': _L0_tok_in['ln_gamma'], 'L0_tok_ln_beta': _L0_tok_in['ln_beta'], 'L0_attn_Wq': _L0_attn_in['Wq'], 'L0_attn_bq': _L0_attn_in['bq'], 'L0_attn_Wk': _L0_attn_in['Wk'], 'L0_attn_bk': _L0_attn_in['bk'], 'L0_attn_Wv': _L0_attn_in['Wv'], 'L0_attn_bv': _L0_attn_in['bv'], 'L0_attn_Wo': _L0_attn_in['Wo'], 'L0_attn_bo': _L0_attn_in['bo'], 'L0_ffn_attention_mask': _L0_ffn_in['attention_mask'], 'L0_ffn_wr': _L0_ffn_in['wr'], 'L0_ffn_br': _L0_ffn_in['br'], 'L0_ffn_w1': _L0_ffn_in['w1'], 'L0_ffn_b1': _L0_ffn_in['b1'], 'L0_ffn_w2': _L0_ffn_in['w2'], 'L0_ffn_b2': _L0_ffn_in['b2']}

def reference(x, L0_tok_emb_table, L0_tok_geo_table, L0_tok_visit_table, L0_tok_w_item, L0_tok_b_item, L0_tok_w_geo, L0_tok_b_geo, L0_tok_w_visit, L0_tok_b_visit, L0_tok_w_fuse, L0_tok_b_fuse, L0_tok_ln_gamma, L0_tok_ln_beta, L0_attn_Wq, L0_attn_bq, L0_attn_Wk, L0_attn_bk, L0_attn_Wv, L0_attn_bv, L0_attn_Wo, L0_attn_bo, L0_ffn_attention_mask, L0_ffn_wr, L0_ffn_br, L0_ffn_w1, L0_ffn_b1, L0_ffn_w2, L0_ffn_b2):
    import jax
    import jax.numpy as jnp

    def _L0_tok_ref(item_ids, emb_table, geo_table, visit_table, w_item, b_item, w_geo, b_geo, w_visit, b_visit, w_fuse, b_fuse, ln_gamma, ln_beta):
        import jax, jax.numpy as jnp
        import numpy as np
        NUM_ITEMS = 25000
        D = 64
        FOURIER_DIM = 64
        VISIT_DIM = 24
        RESIDUAL_SCALE = 0.1
        LN_EPS = 1e-05

        def _layer_norm(x, gamma, beta):
            mu = jnp.mean(x, axis=-1, keepdims=True)
            var = jnp.mean(jnp.square(x - mu), axis=-1, keepdims=True)
            return (x - mu) * jax.lax.rsqrt(var + LN_EPS) * gamma + beta
        gelu = lambda x: jax.nn.gelu(x, approximate=False)
        safe_ids = jnp.clip(item_ids, 0, emb_table.shape[0] - 1)
        item_emb = emb_table[safe_ids]
        fourier_feat = geo_table[safe_ids]
        visit_feat = visit_table[safe_ids]
        item_h = gelu(item_emb @ w_item + b_item)
        geo_h = gelu(fourier_feat @ w_geo + b_geo)
        visit_h = gelu(visit_feat @ w_visit + b_visit)
        cat = jnp.concatenate([item_h, geo_h, visit_h], axis=-1)
        fused = _layer_norm(gelu(cat @ w_fuse + b_fuse), ln_gamma, ln_beta)
        valid_mask = (item_ids != 0)[..., None].astype(fused.dtype)
        fused = fused * valid_mask
        return item_emb + RESIDUAL_SCALE * fused

    def _L0_attn_ref(x, Wq, bq, Wk, bk, Wv, bv, Wo, bo):
        import jax, jax.numpy as jnp
        import numpy as np
        DIM = 64
        HEADS = 4
        HEAD_DIM = DIM // HEADS
        SCALE = HEAD_DIM ** (-0.5)
        B, N, C = x.shape
        x = jnp.clip(x, -10000.0, 10000.0)

        def heads(t):
            return t.reshape(B, N, HEADS, HEAD_DIM).transpose(0, 2, 1, 3)
        q = heads((x @ Wq.T + bq).astype(jnp.float32))
        k = heads((x @ Wk.T + bk).astype(jnp.float32))
        v = heads((x @ Wv.T + bv).astype(jnp.float32))
        attn = jnp.einsum('bhnd,bhmd->bhnm', q, k) * SCALE
        attn = jax.nn.softmax(attn, axis=-1)
        out = jnp.einsum('bhnm,bhmd->bhnd', attn, v)
        out = out.transpose(0, 2, 1, 3).reshape(B, N, C)
        out = out.astype(jnp.bfloat16).astype(jnp.float32)
        return out @ Wo.T + bo

    def _L0_ffn_ref(x, attention_mask, wr, br, w1, b1, w2, b2):
        import jax, jax.numpy as jnp
        import numpy as np
        B, S, D = (8, 1024, 64)
        H = 4 * D
        CAPACITY = 0.5
        b, s, d = x.shape
        weights = (jnp.einsum('bsd,do->bso', x, wr) + br)[..., 0]
        k = max(1, int(CAPACITY * s))
        kk = k - 1 if k > 1 else 1
        _, idx = jax.lax.top_k(weights, k)
        sel_idx = idx[:, :kk]
        sel = jnp.take_along_axis(x, sel_idx[:, :, None], axis=1)
        h = jax.nn.gelu(jnp.einsum('bkd,dh->bkh', sel, w1) + b1)
        y = jnp.einsum('bkh,hd->bkd', h, w2) + b2
        w_sel = jnp.take_along_axis(weights, sel_idx, axis=1)
        y = y * w_sel[..., None]
        batch_idx = jnp.arange(b)[:, None]
        processed = jnp.zeros_like(x).at[batch_idx, sel_idx].set(y)
        return processed + x
    h = _L0_tok_ref(x, L0_tok_emb_table, L0_tok_geo_table, L0_tok_visit_table, L0_tok_w_item, L0_tok_b_item, L0_tok_w_geo, L0_tok_b_geo, L0_tok_w_visit, L0_tok_b_visit, L0_tok_w_fuse, L0_tok_b_fuse, L0_tok_ln_gamma, L0_tok_ln_beta)
    h = h + _L0_attn_ref(_layernorm(h, axis=-1), L0_attn_Wq, L0_attn_bq, L0_attn_Wk, L0_attn_bk, L0_attn_Wv, L0_attn_bv, L0_attn_Wo, L0_attn_bo)
    h = h + _L0_ffn_ref(_layernorm(h, axis=-1), L0_ffn_attention_mask, L0_ffn_wr, L0_ffn_br, L0_ffn_w1, L0_ffn_b1, L0_ffn_w2, L0_ffn_b2)
    return h

_drawn_inputs = setup_inputs


def setup_inputs(seed=0):
    import zlib

    import numpy as np

    out = dict(_drawn_inputs(seed))
    spreads = {'L0_tok_b_item': (0.0, 0.1),
     'L0_tok_b_geo': (0.0, 0.1),
     'L0_tok_b_visit': (0.0, 0.1),
     'L0_tok_b_fuse': (0.0, 0.1),
     'L0_tok_ln_gamma': (1.0, 0.2),
     'L0_tok_ln_beta': (0.0, 0.1),
     'L0_attn_bq': (0.0, 0.652),
     'L0_attn_bk': (0.0, 0.8),
     'L0_attn_bv': (0.0, 0.1),
     'L0_attn_bo': (0.0, 0.1),
     'L0_ffn_b1': (0.0, 0.8),
     'L0_ffn_b2': (0.0, 0.8)}
    factors = {'L0_tok_w_item': 2.709, 'L0_ffn_wr': 8.0, 'L0_ffn_w1': 8.0, 'L0_ffn_w2': 8.0}
    for name, (base, spread) in spreads.items():
        noise = np.random.default_rng([zlib.crc32(name.encode()), seed]).standard_normal(out[name].shape)
        drawn = base * np.exp(spread * noise) if base else spread * noise
        out[name] = jnp.asarray(drawn.astype(out[name].dtype))
    for name, factor in factors.items():
        out[name] = (out[name] * factor).astype(out[name].dtype)
    return out
```

```python
from contextlib import ExitStack

import concourse.bass as bass
from concourse import mybir

F32 = mybir.dt.float32
F32R = mybir.dt.float32r
BF16 = mybir.dt.bfloat16
I32 = mybir.dt.int32
ALU = mybir.AluOpType
ACT = mybir.ActivationFunctionType
AX = mybir.AxisListType.X

P = 128
D = 64
VD = 24
FEAT = 2 * D + VD
HEADS = 4
HD = D // HEADS
HID = 4 * D
GB = 4
NG = P // GB
GT = GB * P
KEEP = P // 2 - 1
LN_EPS = 1e-5
SCALE = HD ** -0.5
LOWEST = -3.0e38
FIRST = 4
OC = 16

_COLS = [
    ("w_q", P), ("w_k", P), ("w_v", D), ("w_1", HID),
    ("w_ig", P), ("w_vi", 2 * P), ("w_fe", P), ("w_fo", P), ("w_fv", P), ("w_2", 2 * D),
    ("w_o", D), ("ident", P),
    ("gamma", D), ("beta", D), ("bv", D), ("b2", D), ("wr", D), ("br", 1),
    ("b_ig", 1), ("b_vi", 1), ("b_fu", 1), ("b_q", 1), ("b_k", 1), ("b_1", 2), ("lo_row", 1),
]
COL, _at = {}, 0
for _n, _c in _COLS:
    COL[_n] = (_at, _at + _c)
    _at += _c
PACKED = _at
SPLIT = COL["w_1"][1]


def build(nc, ids, table, packed, out):
    with ExitStack() as ctx:
        def sb(name, shape, dt=F32):
            return ctx.enter_context(nc.sbuf_tensor(name, shape, dt))

        def sem(name):
            return ctx.enter_context(nc.semaphore(name))

        wt = sb("wt", [P, PACKED])
        w = {n: wt[:, a:b] for n, (a, b) in COL.items()}
        w_hi = sb("w_hi", [P, SPLIT], F32R)
        w_lo = sb("w_lo", [P, SPLIT], F32R)
        hi = {n: w_hi[:, COL[n][0]:COL[n][1]] for n in ("w_q", "w_k", "w_v", "w_1")}
        lo = {n: w_lo[:, COL[n][0]:COL[n][1]] for n in ("w_q", "w_k", "w_v", "w_1")}
        wo_part = sb("wo_part", [P, 3, D], BF16)
        wo_rest = sb("wo_rest", [P, 2, D])
        ident = w["ident"]
        ident_bf = sb("ident_bf", [P, P], BF16)
        ones_r = sb("ones_r", [P, P], F32R)
        g_tenth = sb("g_tenth", [P, D])
        b_tenth = sb("b_tenth", [P, D])
        bq_lo = sb("bq_lo", [P, 1])
        ids_sb = sb("ids_sb", [P, P], I32)
        idx_all = sb("idx_all", [P, P], I32)
        valid = sb("valid", [P, P])

        R = sb("R", [P, P, D])
        Y = sb("Y", [P, P, D])
        W = sb("W", [P, P])

        idx = [sb(f"idx{p}", [P, GB], I32) for p in range(2)]
        G = [sb(f"G{p}", [P, GB, FEAT]) for p in range(2)]
        gv = sb("gv", [P, GB, VD])
        ig_in = sb("ig_in", [P, GT])
        vi_in = sb("vi_in", [P, P])
        cat = sb("cat", [P, GT])
        catv = sb("catv", [P, 2 * P])
        fused = sb("fused", [P, 2 * P])
        st1, st2, st3 = (sb(f"st{n}", [P, GB, 6]) for n in (1, 2, 3))
        mv1, mv2, mv3 = (sb(f"mv{n}", [P, GB, 2]) for n in (1, 2, 3))
        rs1, rs2, rs3 = (sb(f"rs{n}", [P, GB]) for n in (1, 2, 3))
        minus_half = sb("minus_half", [P, GB])
        t1 = sb("t1", [P, GB, D])
        t2 = sb("t2", [P, GB, D])
        u = sb("u", [P, GB, D])
        u0 = sb("u0", [P, GB, D])
        x2 = sb("x2", [P, GB, D])
        x2s = sb("x2s", [P, GB, 2, D], F32R)
        x2t = sb("x2t", [P, GT], F32R)
        q_mask = sb("q_mask", [P, GT])
        q_s = sb("q_s", [P, GT], F32R)
        q_bd = [sb(f"q_bd{p}", [P, GB, HEADS, P], F32R) for p in range(2)]
        k_bd = sb("k_bd", [P, GB, HEADS, P], F32R)
        k_hi = [sb(f"k_hi{p}", [P, GT], F32R) for p in range(2)]
        k_lo = [sb(f"k_lo{p}", [P, GT], F32R) for p in range(2)]
        V = [sb(f"V{p}", [P, GB, HEADS, HD + 1]) for p in range(2)]
        neg_max = sb("neg_max", [P, P])
        max_t = sb("max_t", [GB * HEADS, P], F32R)
        max_row = sb("max_row", [P, GB, HEADS * P], F32R)
        prob = sb("prob", [P, GB, HEADS, P])
        rsum = sb("rsum", [P, GB, HEADS])
        o = sb("o", [P, GB, P], BF16)
        o_t = sb("o_t", [P, GT], BF16)
        x3 = sb("x3", [P, GB, D])
        x3s = sb("x3s", [P, GB, 2, D], F32R)
        x3t = sb("x3t", [P, GT], F32R)
        xw = sb("xw", [P, GB, D])
        hid = sb("hid", [P, 2, GT])
        wt_rank = sb("wt_rank", [P, P])
        left = sb("left", [P, P])
        top = sb("top", [P, 8])
        over = sb("over", [P, P])
        equal = sb("equal", [P, P])
        order = sb("order", [P, P])
        room = sb("room", [P, 1])
        coef_t = sb("coef_t", [P, P])
        coef = sb("coef", [P, P])

        bank = [ctx.enter_context(nc.psum_tensor(f"bank{n}", [P, 512], F32)) for n in range(8)]

        consts_in = sem("consts_in")
        consts_ready = sem("consts_ready")
        zeros_ready = sem("zeros_ready")
        ids_ready = sem("ids_ready")
        gathered = [sem(f"gathered{p}") for p in range(2)]
        S = {n: sem(n) for n in (
            "idx_ready", "gv_ready", "gt_ready", "vt_ready", "gt_out", "vt_out", "ig_ready", "vi_ready",
            "cat_ready", "catv_ready", "fu_ready", "fused_ready", "ft_ready",
            "st1_ready", "mv1_ready", "rs1_ready", "rm1_ready", "t1_ready", "t2_ready",
            "u0_ready", "u_ready", "h1_ready", "st2_ready", "mv2_ready", "rs2_ready", "x2_ready",
            "x2h_ready", "x2s_ready", "xt_ready", "x2t_ready", "q_ready", "k_ready", "v_ready",
            "qm_ready", "qs_ready", "kh_ready", "kl_ready", "v_out", "q_bd_in", "k_bd_in",
            "s_ready", "max_ready", "mt_ready", "max_t_ready", "max_row_in", "st_ready",
            "prob_ready", "pv_ready", "rsum_ready", "o_ready", "ot_ready", "o_t_ready", "wo_ready",
            "h2_ready", "st3_ready", "mv3_ready", "rs3_ready", "x3_ready", "x3h_ready",
            "x3s_ready", "xw_ready", "w_ready", "r_ready", "x3t_ready", "x3t_out", "f1_ready",
            "hid_ready", "f2_ready", "y_ready",
        )}
        wT_ready, topk_step, coefT_ready, cT_ready, coef_ready = (
            sem(n) for n in ("wT_ready", "topk_step", "coefT_ready", "cT_ready", "coef_ready"))
        scaled, summed, pool_scaled, pool_summed = (
            sem(n) for n in ("scaled", "summed", "pool_scaled", "pool_summed"))
        stored = sem("stored")
        passed = sem("passed")

        def wait(eng, name, per, g, k=None, alone=False):
            k = per if k is None else k
            if type(g) is int:
                if g < 0:
                    return
                if g >= NG:
                    g, k = NG - 1, per
            eng.wait_ge(S[name], g * per + k)
            if alone and type(g) is not int:
                eng.sem_inc(passed, 1)

        def on(g):
            return type(g) is not int or 0 <= g < NG

        def of(tile, g):
            return tile[:, bass.ds(g * GB, GB)]

        def pipeline(eng, step, ahead=2):
            turns = (NG - ahead - FIRST) // 2
            for i in range(-2, FIRST):
                step(i, i % 2, i // 2)
            with eng.Fori(0, turns) as t:
                for odd in range(2):
                    step(t * 2 + (FIRST + odd), odd, t + FIRST // 2)
            for i in range(FIRST + 2 * turns, NG + 2):
                step(i, i % 2, i // 2)

        block = ctx.enter_context(nc.Block())

        @block.sync
        def _(sp):
            sp.dma_start(ids_sb[:, :], ids).then_inc(consts_in, 16)
            sp.dma_start(wt[:, :], packed).then_inc(consts_in, 16)
            sp.wait_ge(zeros_ready, 3)

            def step(i, odd, half):
                b, c = i + 1, i
                if on(c):
                    wait(sp, "max_t_ready", 1, c)
                    wait(sp, "st_ready", GB, c - 1)
                    sp.dma_start(max_row[0:1, :, :].rearrange("p b (h q) -> p (b h) q", h=HEADS
                                                              ).bitcast(F32),
                                 max_t[:, :].bitcast(F32)).then_inc(S["max_row_in"], 16)
                if on(b):
                    wait(sp, "qs_ready", 1, b)
                    wait(sp, "st_ready", GB, b - 2)
                    for h in range(HEADS):
                        rows = slice(32 * h, 32 * h + 32)
                        sp.dma_start(q_bd[1 - odd][rows, :, h, :].bitcast(F32),
                                     q_s[rows, :].rearrange("p (b q) -> p b q", b=GB).bitcast(F32)
                                     ).then_inc(S["q_bd_in"], 16)
                    wait(sp, "kh_ready", 1, b)
                    wait(sp, "s_ready", GB, b - 1)
                    for h in range(HEADS):
                        rows = slice(32 * h, 32 * h + 32)
                        sp.dma_start(k_bd[rows, :, h, :].bitcast(F32),
                                     k_hi[1 - odd][rows, :].rearrange("p (b k) -> p b k", b=GB
                                                                      ).bitcast(F32)
                                     ).then_inc(S["k_bd_in"], 16)

            pipeline(sp, step)
            for n in range(P // OC):
                if n % 4 == 3:
                    sp.wait_ge(pool_summed, n // 4 + 1)
                else:
                    sp.wait_ge(summed, n - n // 4 + 1)
                part = slice(n * OC, (n + 1) * OC)
                sp.dma_start(out[part, :, :].rearrange("b t d -> t b d"), R[:, part, :]
                             ).then_inc(stored, 16)
            sp.wait_ge(stored, 16 * (P // OC))

        @block.gpsimd
        def _(pool):
            for p in range(2):
                pool.memset(q_bd[p][:, :, :, :].bitcast(F32), 0.0)
            pool.memset(k_bd[:, :, :, :].bitcast(F32), 0.0)
            pool.memset(max_row[:, :, :].bitcast(F32), 0.0)
            pool.memset(minus_half[:, :], -0.5)
            pool.memset(neg_max[:, :], 0.0)
            pool.memset(o[:, :, :], 0.0).then_inc(zeros_ready, 1)
            pool.wait_ge(zeros_ready, 1)
            pool.memset(o[:, :, D:D + 1], 1.0).then_inc(zeros_ready, 1)
            for p in range(2):
                last = pool.memset(V[p][:, :, :, HD:HD + 1], 1.0)
            last.then_inc(zeros_ready, 1)

            def fetch(g, par, g_half):
                pool.tensor_copy(idx[par][:, :], of(idx_all, g)).then_inc(S["idx_ready"], 1)
                wait(pool, "idx_ready", 1, g, alone=True)
                wait(pool, "gt_ready", 1, g - 2, alone=True)
                wait(pool, "gv_ready", 1, g - 2, alone=True)
                wait(pool, "u_ready", 1, g - 2, alone=True)
                for b in range(GB):
                    pool.indirect_dma_start(
                        G[par][:, b, :], None, table,
                        bass.IndirectOffsetOnAxis(ap=idx[par][:, b:b + 1], axis=0),
                    ).then_inc(gathered[par], 16)

            def rstd(mv, rs, src, dst, g):
                wait(pool, src, 1, g, alone=True)
                pool.tensor_scalar(rs[:, :], mv[:, :, 1], LN_EPS, None, ALU.add
                                   ).then_inc(S[dst], 1)
                wait(pool, dst, 2, g, 1, alone=True)
                pool.tensor_tensor(rs[:, :], rs[:, :], minus_half[:, :], ALU.pow
                                   ).then_inc(S[dst], 1)

            pool.wait_ge(ids_ready, 2)
            pool.wait_ge(consts_ready, 1)
            pool.wait_ge(zeros_ready, 3)
            fetch(0, 0, 0)

            def step(i, odd, half):
                a, e = i + 2, i - 1
                nxt = i + 3
                if on(a):
                    pool.wait_ge(gathered[odd], (half + 1) * 64 + 64)
                    wait(pool, "vt_ready", 1, a - 1, alone=True)
                    pool.tensor_copy(gv[:, :, :], G[odd][:, :, 2 * D:FEAT]
                                     ).then_inc(S["gv_ready"], 1)
                if on(nxt):
                    fetch(nxt, 1 - odd, None)
                if on(a):
                    wait(pool, "h1_ready", 1, a - 1, alone=True)
                    pool.tensor_tensor(
                        u0[:, :, :], of(valid, a).unsqueeze(2).to_broadcast([P, GB, D]),
                        b_tenth[:, :].unsqueeze(1).to_broadcast([P, GB, D]), ALU.mult
                    ).then_inc(S["u0_ready"], 1)
                    wait(pool, "u0_ready", 1, a, alone=True)
                    pool.tensor_tensor(u[:, :, :], u0[:, :, :], G[odd][:, :, 0:D], ALU.add
                                       ).then_inc(S["u_ready"], 1)
                    rstd(mv1, rs1, "mv1_ready", "rs1_ready", a)
                    wait(pool, "rs1_ready", 2, a, alone=True)
                    pool.tensor_tensor(rs1[:, :], rs1[:, :], of(valid, a), ALU.mult
                                       ).then_inc(S["rm1_ready"], 1)
                    rstd(mv2, rs2, "mv2_ready", "rs2_ready", a)
                if on(e):
                    rstd(mv3, rs3, "mv3_ready", "rs3_ready", e)
                    wait(pool, "x3_ready", 1, e, alone=True)
                    wait(pool, "w_ready", 1, e - 1, alone=True)
                    pool.tensor_tensor(xw[:, :, :], x3[:, :, :],
                                       w["wr"].unsqueeze(1).to_broadcast([P, GB, D]), ALU.mult
                                       ).then_inc(S["xw_ready"], 1)
                    wait(pool, "st3_ready", 1, e, alone=True)
                    pool.tensor_tensor(of(R, e), of(R, e), x3[:, :, :], ALU.add
                                       ).then_inc(S["r_ready"], 1)

            pipeline(pool, step, ahead=3)
            pool.wait_ge(coef_ready, 1)
            wait(pool, "y_ready", 1, NG - 1, alone=True)
            wait(pool, "r_ready", 1, NG - 1, alone=True)
            for m, n in enumerate(range(3, P // OC, 4)):
                part = slice(n * OC, (n + 1) * OC)
                pool.tensor_tensor(Y[:, part, :], Y[:, part, :],
                                   coef[:, part].unsqueeze(2).to_broadcast([P, OC, D]), ALU.mult
                                   ).then_inc(pool_scaled, 1)
                pool.wait_ge(pool_scaled, m + 1)
                pool.tensor_tensor(R[:, part, :], R[:, part, :], Y[:, part, :], ALU.add
                                   ).then_inc(pool_summed, 1)

        @block.scalar
        def _(act):
            act.wait_ge(consts_ready, 1)
            act.wait_ge(zeros_ready, 3)

            def step(i, odd, half):
                a, b, c, e, d = i + 2, i + 1, i, i - 1, i - 2
                if on(a):
                    wait(act, "gt_ready", 1, a)
                    act.activation(ig_in[:, :], bank[4][:, :], ACT.Copy).then_inc(S["gt_out"], 1)
                    wait(act, "ig_ready", 1, a)
                    act.activation(cat[:, :], bank[6][:, :], ACT.Gelu, bias=w["b_ig"]
                                   ).then_inc(S["cat_ready"], 1)
                    wait(act, "vi_ready", 1, a)
                    act.activation(catv[:, :], bank[7][:, 0:2 * P], ACT.Gelu, bias=w["b_vi"]
                                   ).then_inc(S["catv_ready"], 1)
                if on(b):
                    wait(act, "xt_ready", 1, b)
                    wait(act, "v_ready", 1, b - 1)
                    act.activation(x2t[:, :], bank[4][:, :], ACT.Copy).then_inc(S["x2t_ready"], 1)
                if on(d):
                    wait(act, "x3t_ready", 1, d)
                    act.activation(x3t[:, :], bank[5][:, :], ACT.Copy).then_inc(S["x3t_out"], 1)
                if on(a):
                    wait(act, "fu_ready", 1, a)
                    wait(act, "ft_ready", 1, a - 1)
                    act.activation(fused[:, :], bank[7][:, 0:2 * P], ACT.Gelu, bias=w["b_fu"]
                                   ).then_inc(S["fused_ready"], 1)
                if on(d):
                    for m in range(2):
                        wait(act, "f1_ready", 2, d, m + 1)
                        if m == 0:
                            wait(act, "f2_ready", 1, d - 1)
                        act.activation(hid[:, m, :], bank[4 + m][:, :], ACT.Gelu_apprx_tanh,
                                       bias=w["b_1"][:, m:m + 1]).then_inc(S["hid_ready"], 1)
                if on(b):
                    wait(act, "q_ready", 1, b)
                    wait(act, "qs_ready", 1, b - 1)
                    act.activation(q_mask[:, :].bitcast(F32R), bank[6][:, :], ACT.Identity,
                                   bias=bq_lo[:, :], scale=w["lo_row"]).then_inc(S["qm_ready"], 1)
                    wait(act, "k_ready", 1, b)
                    wait(act, "st_ready", GB, b - 2)
                    wait(act, "k_bd_in", 64, b - 2)
                    act.activation(k_hi[1 - odd][:, :], bank[4][:, :], ACT.Identity,
                                   bias=w["b_k"]).then_inc(S["kh_ready"], 1)
                if on(c):
                    for s in range(GB):
                        wait(act, "st_ready", GB, c, s + 1)
                        if s == 0:
                            wait(act, "pv_ready", 1, c - 1)
                        act.activation(prob[:, s, :, :].rearrange("p h q -> p (h q)"),
                                       bank[s][:, :], ACT.Exp, scale=SCALE
                                       ).then_inc(S["prob_ready"], 1)
                if on(e):
                    wait(act, "ot_ready", 1, e)
                    wait(act, "wo_ready", 1, e - 1)
                    act.activation(o_t[:, :], bank[5][:, 0:GT // 2].bitcast(BF16), ACT.Copy
                                   ).then_inc(S["o_t_ready"], 1)

            pipeline(act, step)

        @block.vector
        def _(dve):
            dve.wait_ge(consts_in, 32)
            dve.tensor_scalar(idx_all[:, :], ids_sb[:, :], 0, 25000, ALU.max, ALU.min
                              ).then_inc(ids_ready, 1)
            dve.tensor_scalar(valid[:, :], ids_sb[:, :], 0, None, ALU.not_equal
                              ).then_inc(ids_ready, 1)
            dve.memset(ones_r[:, :].bitcast(F32), 1.0)
            dve.tensor_copy(w_hi[:, :], wt[:, 0:SPLIT])
            dve.tensor_copy(wo_part[:, 0, :], w["w_o"])
            dve.tensor_copy(ident_bf[:, :], ident)
            dve.tensor_scalar(g_tenth[:, :], w["gamma"], 0.1, None, ALU.mult)
            dve.tensor_scalar(b_tenth[:, :], w["beta"], 0.1, None, ALU.mult)
            dve.tensor_tensor(bq_lo[:, :], w["b_q"], w["lo_row"], ALU.mult).then_inc(topk_step, 1)
            dve.wait_ge(topk_step, 1)
            dve.tensor_tensor(w_lo[:, :], wt[:, 0:SPLIT], w_hi[:, :].bitcast(F32), ALU.subtract)
            dve.tensor_tensor(wo_rest[:, 0, :], w["w_o"], wo_part[:, 0, :], ALU.subtract
                              ).then_inc(topk_step, 1)
            dve.wait_ge(topk_step, 2)
            dve.tensor_copy(wo_part[:, 1, :], wo_rest[:, 0, :]).then_inc(topk_step, 1)
            dve.wait_ge(topk_step, 3)
            dve.tensor_tensor(wo_rest[:, 1, :], wo_rest[:, 0, :], wo_part[:, 1, :], ALU.subtract
                              ).then_inc(topk_step, 1)
            dve.wait_ge(topk_step, 4)
            dve.tensor_copy(wo_part[:, 2, :], wo_rest[:, 1, :]).then_inc(consts_ready, 1)
            setup_steps = 4
            dve.wait_ge(consts_ready, 1)
            dve.wait_ge(zeros_ready, 3)

            def stats(src, st, mv, st_done, mv_done, g):
                for b in range(GB):
                    last = dve.bn_stats(st[:, b, :], src(b))
                last.then_inc(S[st_done], 1)
                wait(dve, st_done, 1, g, alone=True)
                for b in range(GB):
                    last = dve.bn_aggr(mv[:, b, :], st[:, b, :])
                last.then_inc(S[mv_done], 1)

            def normalize(dst, src, mv, rs, done, g):
                for b in range(GB):
                    last = dve.tensor_scalar(dst[:, b, :], src(b), mv[:, b, 0:1], rs[:, b:b + 1],
                                             ALU.subtract, ALU.mult)
                last.then_inc(S[done], 1)

            def split(dst, src, hi_done, lo_done, g):
                dve.tensor_copy(dst[:, :, 0, :], src[:, :, :]).then_inc(S[hi_done], 1)
                wait(dve, hi_done, 1, g)
                dve.tensor_tensor(dst[:, :, 1, :], src[:, :, :], dst[:, :, 0, :].bitcast(F32),
                                  ALU.subtract).then_inc(S[lo_done], 1)

            def step(i, odd, half):
                a, b, c, e, d = i + 2, i + 1, i, i - 1, i - 2
                if on(a):
                    wait(dve, "vt_ready", 1, a)
                    wait(dve, "vi_ready", 1, a - 1)
                    dve.tensor_copy(vi_in[0:GB * VD, :], bank[5][0:GB * VD, 0:P]
                                    ).then_inc(S["vt_out"], 1)
                if on(c):
                    for s in range(GB):
                        wait(dve, "s_ready", GB, c, s + 1)
                        dve.tensor_reduce(neg_max[:, HEADS * s:HEADS * s + HEADS],
                                          bank[s][:, :].rearrange("p (h k) -> p h k", h=HEADS),
                                          AX, ALU.max, negate=True).then_inc(S["max_ready"], 1)
                    wait(dve, "mt_ready", 1, c)
                    wait(dve, "max_row_in", 16, c - 1)
                    dve.tensor_copy(max_t[:, :], bank[0][0:GB * HEADS, 0:P]
                                    ).then_inc(S["max_t_ready"], 1)
                if on(e):
                    pv = bank[6][:, 0:GB * HEADS * (HD + 1)].rearrange(
                        "p (b h d) -> p b h d", b=GB, h=HEADS)
                    wait(dve, "pv_ready", 1, e)
                    dve.reciprocal(rsum[:, :, :], pv[:, :, :, HD]).then_inc(S["rsum_ready"], 1)
                    wait(dve, "rsum_ready", 1, e)
                    wait(dve, "ot_ready", 1, e - 1)
                    dve.tensor_tensor(
                        o[:, :, 0:D].rearrange("p b (h d) -> p b h d", h=HEADS), pv[:, :, :, 0:HD],
                        rsum[:, :, :].unsqueeze(3).to_broadcast([P, GB, HEADS, HD]), ALU.mult
                    ).then_inc(S["o_ready"], 1)
                if on(b):
                    wait(dve, "qm_ready", 1, b)
                    wait(dve, "q_bd_in", 64, b - 1)
                    wait(dve, "s_ready", GB, b - 1)
                    dve.scalar_tensor_tensor(q_s[:, :], bank[6][:, :], w["b_q"], q_mask[:, :],
                                             ALU.add, ALU.subtract).then_inc(S["qs_ready"], 1)
                    wait(dve, "kh_ready", 1, b)
                    wait(dve, "st_ready", GB, b - 2)
                    dve.scalar_tensor_tensor(k_lo[1 - odd][:, :], bank[4][:, :], w["b_k"],
                                             k_hi[1 - odd][:, :].bitcast(F32),
                                             ALU.add, ALU.subtract).then_inc(S["kl_ready"], 1)
                if on(d):
                    wait(dve, "f2_ready", 1, d)
                    dve.tensor_tensor(
                        of(Y, d), bank[6][:, 0:GB * D].rearrange("p (b d) -> p b d", b=GB),
                        w["b2"].unsqueeze(1).to_broadcast([P, GB, D]), ALU.add
                    ).then_inc(S["y_ready"], 1)
                if on(b):
                    wait(dve, "v_ready", 1, b)
                    wait(dve, "pv_ready", 1, b - 2)
                    dve.tensor_tensor(
                        V[1 - odd][:, :, :, 0:HD],
                        bank[0][:, 0:GB * D].rearrange("p (b h d) -> p b h d", b=GB, h=HEADS),
                        w["bv"].rearrange("p (h d) -> p h d", h=HEADS).unsqueeze(1).to_broadcast(
                            [P, GB, HEADS, HD]), ALU.add).then_inc(S["v_out"], 1)
                if on(a):
                    ft = bank[7][:, 0:GB * D].rearrange("p (b d) -> p b d", b=GB)
                    wait(dve, "ft_ready", 1, a, alone=True)
                    stats(lambda s: ft[:, s, :], st1, mv1, "st1_ready", "mv1_ready", a)
                    wait(dve, "rm1_ready", 1, a)
                    normalize(t1, lambda s: ft[:, s, :], mv1, rs1, "t1_ready", a)
                    wait(dve, "t1_ready", 1, a)
                    dve.tensor_tensor(t2[:, :, :], t1[:, :, :],
                                      g_tenth[:, :].unsqueeze(1).to_broadcast([P, GB, D]), ALU.mult
                                      ).then_inc(S["t2_ready"], 1)
                    wait(dve, "t2_ready", 1, a)
                    wait(dve, "u_ready", 1, a)
                    dve.tensor_tensor(of(R, a), t2[:, :, :], u[:, :, :], ALU.add
                                      ).then_inc(S["h1_ready"], 1)
                    wait(dve, "h1_ready", 1, a, alone=True)
                    stats(lambda s: R[:, bass.ds(a * GB + s, 1), :].rearrange("p b d -> p (b d)"),
                          st2, mv2, "st2_ready", "mv2_ready", a)
                    wait(dve, "rs2_ready", 2, a)
                    normalize(x2, lambda s: R[:, bass.ds(a * GB + s, 1), :].rearrange(
                        "p b d -> p (b d)"), mv2, rs2, "x2_ready", a)
                    wait(dve, "x2_ready", 1, a)
                    wait(dve, "xt_ready", 1, a - 1)
                    split(x2s, x2, "x2h_ready", "x2s_ready", a)
                if on(e):
                    wait(dve, "wo_ready", 1, e)
                    dve.tensor_tensor(of(R, e), of(R, e),
                                      bank[1][:, 0:GB * D].rearrange("p (b d) -> p b d", b=GB),
                                      ALU.add).then_inc(S["h2_ready"], 1)
                    wait(dve, "h2_ready", 1, e, alone=True)
                    stats(lambda s: R[:, bass.ds(e * GB + s, 1), :].rearrange("p b d -> p (b d)"),
                          st3, mv3, "st3_ready", "mv3_ready", e)
                    wait(dve, "rs3_ready", 2, e)
                    wait(dve, "r_ready", 1, e - 1)
                    normalize(x3, lambda s: R[:, bass.ds(e * GB + s, 1), :].rearrange(
                        "p b d -> p (b d)"), mv3, rs3, "x3_ready", e)
                    wait(dve, "x3_ready", 1, e)
                    wait(dve, "x3t_ready", 1, e - 1)
                    split(x3s, x3, "x3h_ready", "x3s_ready", e)
                    wait(dve, "xw_ready", 1, e)
                    dve.tensor_reduce(of(W, e), xw[:, :, :], AX, ALU.add
                                      ).then_inc(S["w_ready"], 1)

            pipeline(dve, step)

            n = [setup_steps]

            def done(ins):
                n[0] += 1
                ins.then_inc(topk_step, 1)
                dve.wait_ge(topk_step, n[0])

            dve.wait_ge(wT_ready, 1)
            done(dve.tensor_scalar(wt_rank[:, :], bank[0][:, 0:P], w["br"], None, ALU.add))
            done(dve.tensor_copy(left[:, :], wt_rank[:, :]))
            for _ in range(KEEP // 8):
                done(dve.max(top[:, :], left[:, :]))
                done(dve.match_replace(left[:, :], top[:, :], left[:, :], LOWEST))
            done(dve.max(top[:, :], left[:, :]))
            least = top[:, KEEP % 8 - 1:KEEP % 8]
            done(dve.tensor_scalar(over[:, :], wt_rank[:, :], least, None, ALU.is_gt))
            done(dve.tensor_scalar(equal[:, :], wt_rank[:, :], least, None, ALU.is_equal))
            done(dve.tensor_tensor_scan(order[:, :], ones_r[:, :].bitcast(F32), equal[:, :], 0.0,
                                        ALU.mult, ALU.add))
            done(dve.tensor_reduce(room[:, :], over[:, :], AX, ALU.add, negate=True))
            done(dve.tensor_scalar(room[:, :], room[:, :], float(KEEP), None, ALU.add))
            done(dve.scalar_tensor_tensor(order[:, :], order[:, :], room[:, :], equal[:, :],
                                          ALU.is_le, ALU.mult))
            done(dve.tensor_tensor(order[:, :], order[:, :], over[:, :], ALU.add))
            dve.tensor_tensor(coef_t[:, :], order[:, :], wt_rank[:, :], ALU.mult
                              ).then_inc(coefT_ready, 1)
            dve.wait_ge(cT_ready, 1)
            dve.tensor_copy(coef[:, :], bank[1][:, 0:P]).then_inc(coef_ready, 1)
            dve.wait_ge(coef_ready, 1)
            wait(dve, "r_ready", 1, NG - 1)
            m = 0
            for k in range(P // OC):
                if k % 4 == 3:
                    continue
                part = slice(k * OC, (k + 1) * OC)
                dve.tensor_tensor(Y[:, part, :], Y[:, part, :],
                                  coef[:, part].unsqueeze(2).to_broadcast([P, OC, D]), ALU.mult
                                  ).then_inc(scaled, 1)
                m += 1
                dve.wait_ge(scaled, m)
                dve.tensor_tensor(R[:, part, :], R[:, part, :], Y[:, part, :], ALU.add
                                  ).then_inc(summed, 1)

        @block.tensor
        def _(pe):
            pe.wait_ge(consts_ready, 1)
            pe.wait_ge(zeros_ready, 3)
            mm = nc.tensor.matmul

            def step(i, odd, half):
                a, b, c, e, d = i + 2, i + 1, i, i - 1, i - 2
                if on(a):
                    pe.wait_ge(gathered[odd], (half + 1) * 64 + 64)
                    wait(pe, "kl_ready", 1, a - 2)
                    for s in range(GB):
                        last = mm(bank[4][:, s * P:(s + 1) * P], G[odd][:, s, 0:2 * D], ident,
                                  start=True, stop=True, is_transpose=True)
                    last.then_inc(S["gt_ready"], 1)
                    wait(pe, "gv_ready", 1, a)
                    wait(pe, "o_t_ready", 1, a - 4)
                    mm(bank[5][0:GB * VD, 0:P], gv[:, :, :].rearrange("p b d -> p (b d)"), ident,
                       start=True, stop=True, is_transpose=True).then_inc(S["vt_ready"], 1)
                if on(c):
                    wait(pe, "k_bd_in", 64, c)
                    wait(pe, "q_bd_in", 64, c)
                    wait(pe, "kl_ready", 1, c)
                    wait(pe, "v_out", 1, c)
                    wait(pe, "h2_ready", 1, c - 2)
                    wait(pe, "prob_ready", GB, c - 1)
                    for s in range(GB):
                        mm(bank[s][:, :], q_s[:, s * P:(s + 1) * P],
                           k_bd[:, s, :, :].rearrange("p h k -> p (h k)"), start=True, stop=True
                           ).then_inc(S["s_ready"], 1)
                if on(a):
                    wait(pe, "gt_out", 1, a)
                    wait(pe, "y_ready", 1, a - 5)
                    mm(bank[6][:, :], w["w_ig"], ig_in[:, :], start=True, stop=True
                       ).then_inc(S["ig_ready"], 1)
                    wait(pe, "vt_out", 1, a)
                    wait(pe, "t1_ready", 1, a - 1)
                    for n in range(2):
                        last = mm(bank[7][:, n * P:(n + 1) * P],
                                  w["w_vi"][0:GB * VD, n * P:(n + 1) * P], vi_in[0:GB * VD, :],
                                  start=True, stop=True)
                    last.then_inc(S["vi_ready"], 1)
                if on(b):
                    wait(pe, "x2s_ready", 1, b)
                    wait(pe, "gt_out", 1, b + 1)
                    for s in range(GB):
                        last = mm(bank[4][:, s * P:(s + 1) * P],
                                  x2s[:, s, :, :].rearrange("p k d -> p (k d)").bitcast(F32),
                                  ident, start=True, stop=True, is_transpose=True)
                    last.then_inc(S["xt_ready"], 1)
                if on(d):
                    wait(pe, "x3s_ready", 1, d)
                    wait(pe, "vt_out", 1, d + 4)
                    for s in range(GB):
                        last = mm(bank[5][:, s * P:(s + 1) * P],
                                  x3s[:, s, :, :].rearrange("p k d -> p (k d)").bitcast(F32),
                                  ident, start=True, stop=True, is_transpose=True)
                    last.then_inc(S["x3t_ready"], 1)
                if on(c):
                    wait(pe, "max_ready", GB, c)
                    mm(bank[0][:, 0:P], neg_max[:, :], ident, start=True, stop=True,
                       is_transpose=True).then_inc(S["mt_ready"], 1)
                if on(e):
                    wait(pe, "prob_ready", GB, e)
                    wait(pe, "v_out", 1, e)
                    wait(pe, "cat_ready", 1, e + 3)
                    for s in range(GB):
                        for h in range(HEADS):
                            at = (s * HEADS + h) * (HD + 1)
                            last = mm(bank[6][:, at:at + HD + 1], prob[:, s, h, :],
                                      V[1 - odd][:, s, h, :], start=True, stop=True)
                    last.then_inc(S["pv_ready"], 1)
                if on(a):
                    wait(pe, "catv_ready", 1, a)
                    mm(bank[7][:, 0:2 * P], w["w_fv"], catv[:, :], start=True, stop=False)
                    for n, wf in enumerate(("w_fe", "w_fo")):
                        last = mm(bank[7][:, 0:2 * P], w[wf],
                                  cat[:, :].rearrange("p (r s q) -> p s r q", r=2, s=2)[:, n],
                                  start=False, stop=(n == 1))
                    last.then_inc(S["fu_ready"], 1)
                if on(d):
                    wait(pe, "x3t_out", 1, d)
                    wait(pe, "x2t_ready", 1, d + 3)
                    for m in range(2):
                        cols = slice(m * P, (m + 1) * P)
                        mm(bank[4 + m][:, :], hi["w_1"][:, cols], x3t[:, :], start=True, stop=False)
                        mm(bank[4 + m][:, :], lo["w_1"][:, cols], x3t[:, :], start=False, stop=True
                           ).then_inc(S["f1_ready"], 1)
                if on(b):
                    wait(pe, "x2t_ready", 1, b)
                    wait(pe, "o_ready", 1, b - 2)
                    mm(bank[6][:, :], hi["w_q"], x2t[:, :], start=True, stop=False)
                    mm(bank[6][:, :], lo["w_q"], x2t[:, :], start=False, stop=True
                       ).then_inc(S["q_ready"], 1)
                    wait(pe, "hid_ready", 2, b - 3, 1)
                    mm(bank[4][:, :], hi["w_k"], x2t[:, :], start=True, stop=False)
                    mm(bank[4][:, :], lo["w_k"], x2t[:, :], start=False, stop=True
                       ).then_inc(S["k_ready"], 1)
                if on(c):
                    wait(pe, "max_row_in", 16, c)
                    for s in range(GB):
                        tok = slice(s * P, (s + 1) * P)
                        q = q_bd[odd][:, s, :, :].rearrange("p h q -> p (h q)")
                        mm(bank[s][:, :], k_hi[odd][:, tok], q, start=True, stop=False)
                        mm(bank[s][:, :], k_lo[odd][:, tok], q, start=False, stop=False)
                        mm(bank[s][:, :], ones_r[:, :], max_row[:, s, :], start=False, stop=True
                           ).then_inc(S["st_ready"], 1)
                if on(e):
                    wait(pe, "o_ready", 1, e)
                    wait(pe, "hid_ready", 2, e - 1)
                    for s in range(GB):
                        last = mm(bank[5][:, s * P // 2:(s + 1) * P // 2].bitcast(BF16),
                                  o[:, s, :], ident_bf[:, :], start=True, stop=True,
                                  is_transpose=True)
                    last.then_inc(S["ot_ready"], 1)
                if on(d):
                    wait(pe, "hid_ready", 2, d)
                    wait(pe, "qs_ready", 1, d + 3)
                    for s in range(GB):
                        for m in range(2):
                            last = mm(bank[6][:, s * D:(s + 1) * D], hid[:, m, s * P:(s + 1) * P],
                                      w["w_2"][:, m * D:(m + 1) * D], start=(m == 0), stop=(m == 1))
                    last.then_inc(S["f2_ready"], 1)
                if on(b):
                    wait(pe, "prob_ready", GB, b - 1, 1)
                    for s in range(GB):
                        xs = x2t[:, s * P:(s + 1) * P]
                        mm(bank[0][:, s * D:(s + 1) * D], xs, hi["w_v"], start=True, stop=False)
                        last = mm(bank[0][:, s * D:(s + 1) * D], xs, lo["w_v"],
                                  start=False, stop=True)
                    last.then_inc(S["v_ready"], 1)
                if on(a):
                    wait(pe, "fused_ready", 1, a)
                    for n in range(2):
                        last = mm(bank[7][:, n * P:(n + 1) * P], fused[:, n * P:(n + 1) * P],
                                  ident, start=True, stop=True, is_transpose=True)
                    last.then_inc(S["ft_ready"], 1)
                if on(e):
                    wait(pe, "o_t_ready", 1, e)
                    wait(pe, "prob_ready", GB, e + 1, 2)
                    for s in range(GB):
                        for n in range(3):
                            last = mm(bank[1][:, s * D:(s + 1) * D],
                                      o_t[0:D + 1, s * P:(s + 1) * P], wo_part[0:D + 1, n, :],
                                      start=(n == 0), stop=(n == 2))
                    last.then_inc(S["wo_ready"], 1)

            pipeline(pe, step)
            wait(pe, "w_ready", 1, NG - 1)
            mm(bank[0][:, 0:P], W[:, :], ident, start=True, stop=True, is_transpose=True
               ).then_inc(wT_ready, 1)
            pe.wait_ge(coefT_ready, 1)
            mm(bank[1][:, 0:P], coef_t[:, :], ident, start=True, stop=True, is_transpose=True
               ).then_inc(cT_ready, 1)


def kernel(x, L0_tok_emb_table, L0_tok_geo_table, L0_tok_visit_table, L0_tok_w_item,
           L0_tok_b_item, L0_tok_w_geo, L0_tok_b_geo, L0_tok_w_visit, L0_tok_b_visit,
           L0_tok_w_fuse, L0_tok_b_fuse, L0_tok_ln_gamma, L0_tok_ln_beta, L0_attn_Wq, L0_attn_bq,
           L0_attn_Wk, L0_attn_bk, L0_attn_Wv, L0_attn_bv, L0_attn_Wo, L0_attn_bo,
           L0_ffn_attention_mask, L0_ffn_wr, L0_ffn_br, L0_ffn_w1, L0_ffn_b1, L0_ffn_w2,
           L0_ffn_b2):
    import numpy as np
    import concourse.bacc as bacc
    from concourse.bass_utils import run_bass_kernel_spmd

    c = {n: np.zeros((P, b - a), np.float32) for n, (a, b) in COL.items()}

    def per_head(wt):
        wt = wt.reshape(wt.shape[0], HEADS, 1, HD)
        return np.broadcast_to(wt, (wt.shape[0], HEADS, 2, HD)).reshape(wt.shape[0], P)

    for n, src in (("w_q", L0_attn_Wq), ("w_k", L0_attn_Wk)):
        c[n][:D] = c[n][D:] = per_head(np.asarray(src).T)
    c["w_v"][:D] = c["w_v"][D:] = np.asarray(L0_attn_Wv).T
    c["w_1"][:D] = c["w_1"][D:] = np.asarray(L0_ffn_w1)
    c["w_ig"][:D, :D] = np.asarray(L0_tok_w_item)
    c["w_ig"][D:, D:] = np.asarray(L0_tok_w_geo)
    for s in range(GB):
        at = (s // 2) * P + (s % 2) * D
        c["w_vi"][s * VD:(s + 1) * VD, at:at + D] = np.asarray(L0_tok_w_visit)
    wf = np.asarray(L0_tok_w_fuse)
    c["w_fe"][:, :D] = c["w_fo"][:, D:] = wf[:P]
    c["w_fv"][:D, :D] = c["w_fv"][D:, D:] = wf[P:]
    c["w_2"][:, :D], c["w_2"][:, D:] = np.asarray(L0_ffn_w2)[:P], np.asarray(L0_ffn_w2)[P:]
    c["w_o"][:D], c["w_o"][D] = np.asarray(L0_attn_Wo).T, np.asarray(L0_attn_bo)
    c["ident"][:] = np.eye(P, dtype=np.float32)
    for n, src in (("gamma", L0_tok_ln_gamma), ("beta", L0_tok_ln_beta), ("bv", L0_attn_bv),
                   ("b2", L0_ffn_b2), ("wr", L0_ffn_wr), ("br", L0_ffn_br)):
        c[n][:] = np.asarray(src).reshape(1, -1)
    c["b_ig"][:D, 0], c["b_ig"][D:, 0] = np.asarray(L0_tok_b_item), np.asarray(L0_tok_b_geo)
    for n, src in (("b_vi", L0_tok_b_visit), ("b_fu", L0_tok_b_fuse)):
        c[n][:D, 0] = c[n][D:, 0] = np.asarray(src)
    for n, src in (("b_q", L0_attn_bq), ("b_k", L0_attn_bk)):
        c[n][:, 0] = per_head(np.asarray(src).reshape(1, D))[0]
    c["b_1"][:, 0], c["b_1"][:, 1] = np.asarray(L0_ffn_b1)[:P], np.asarray(L0_ffn_b1)[P:]
    c["lo_row"][:, 0] = np.arange(P) // HD % 2

    arrays = {
        "ids": np.ascontiguousarray(np.asarray(x).T),
        "table": np.concatenate([np.asarray(L0_tok_emb_table), np.asarray(L0_tok_geo_table),
                                 np.asarray(L0_tok_visit_table)], axis=1),
        "packed": np.concatenate([c[n] for n, _ in _COLS], axis=1),
    }
    nc = bacc.Bacc("TRN2", target_bir_lowering=False, num_devices=1)
    args = [nc.dram_tensor(n, a.shape, mybir.dt.from_np(a.dtype), kind="ExternalInput").ap()
            for n, a in arrays.items()]
    out = nc.dram_tensor("out", (P, P, D), F32, kind="ExternalOutput").ap()
    build(nc, *args, out)
    r = run_bass_kernel_spmd(nc, [arrays], core_ids=[0])
    return r.results[0]["out"]
```

```python
from contextlib import ExitStack

import concourse.bass as bass
from concourse import mybir

F32 = mybir.dt.float32
F32R = mybir.dt.float32r
BF16 = mybir.dt.bfloat16
I32 = mybir.dt.int32
ALU = mybir.AluOpType
ACT = mybir.ActivationFunctionType
AX = mybir.AxisListType.X

P = 128
D = 64
VD = 24
FEAT = 2 * D + VD
HEADS = 4
HD = D // HEADS
HID = 4 * D
GB = 4
NG = P // GB
GT = GB * P
KEEP = P // 2 - 1
LN_EPS = 1e-5
SCALE = HD ** -0.5
LOWEST = -3.0e38
FIRST = 4
OC = 16

_COLS = [
    ("w_q", P), ("w_k", P), ("w_v", D), ("w_1", HID),
    ("w_ig", P), ("w_vi", 2 * P), ("w_fe", P), ("w_fo", P), ("w_fv", P), ("w_2", 2 * D),
    ("w_o", D), ("ident", P),
    ("gamma", D), ("beta", D), ("bv", D), ("b2", D), ("wr", D), ("br", 1),
    ("b_ig", 1), ("b_vi", 1), ("b_fu", 1), ("b_q", 1), ("b_k", 1), ("b_1", 2), ("lo_row", 1),
]
COL, _at = {}, 0
for _n, _c in _COLS:
    COL[_n] = (_at, _at + _c)
    _at += _c
PACKED = _at
SPLIT = COL["w_1"][1]


def build(nc, ids, table, packed, out):
    with ExitStack() as ctx:
        def sb(name, shape, dt=F32):
            return ctx.enter_context(nc.sbuf_tensor(name, shape, dt))

        def sem(name):
            return ctx.enter_context(nc.semaphore(name))

        wt = sb("wt", [P, PACKED])
        w = {n: wt[:, a:b] for n, (a, b) in COL.items()}
        w_hi = sb("w_hi", [P, SPLIT], F32R)
        w_lo = sb("w_lo", [P, SPLIT], F32R)
        hi = {n: w_hi[:, COL[n][0]:COL[n][1]] for n in ("w_q", "w_k", "w_v", "w_1")}
        lo = {n: w_lo[:, COL[n][0]:COL[n][1]] for n in ("w_q", "w_k", "w_v", "w_1")}
        wo_part = sb("wo_part", [P, 3, D], BF16)
        wo_rest = sb("wo_rest", [P, 2, D])
        ident = w["ident"]
        ident_bf = sb("ident_bf", [P, P], BF16)
        ones_r = sb("ones_r", [P, P], F32R)
        g_tenth = sb("g_tenth", [P, D])
        b_tenth = sb("b_tenth", [P, D])
        bq_lo = sb("bq_lo", [P, 1])
        ids_sb = sb("ids_sb", [P, P], I32)
        idx_all = sb("idx_all", [P, P], I32)
        valid = sb("valid", [P, P])

        R = sb("R", [P, P, D])
        Y = sb("Y", [P, P, D])
        W = sb("W", [P, P])

        idx = [sb(f"idx{p}", [P, GB], I32) for p in range(2)]
        G = [sb(f"G{p}", [P, GB, FEAT]) for p in range(2)]
        gv = sb("gv", [P, GB, VD])
        ig_in = sb("ig_in", [P, GT])
        vi_in = sb("vi_in", [P, P])
        cat = sb("cat", [P, GT])
        catv = sb("catv", [P, 2 * P])
        fused = sb("fused", [P, 2 * P])
        st1, st2, st3 = (sb(f"st{n}", [P, GB, 6]) for n in (1, 2, 3))
        mv1, mv2, mv3 = (sb(f"mv{n}", [P, GB, 2]) for n in (1, 2, 3))
        rs1, rs2, rs3 = (sb(f"rs{n}", [P, GB]) for n in (1, 2, 3))
        minus_half = sb("minus_half", [P, GB])
        t1 = sb("t1", [P, GB, D])
        u = sb("u", [P, GB, D])
        u0 = sb("u0", [P, GB, D])
        x2 = sb("x2", [P, GB, D])
        x2s = sb("x2s", [P, GB, 2, D], F32R)
        x2t = sb("x2t", [P, GT], F32R)
        q_mask = sb("q_mask", [P, GT])
        q_s = sb("q_s", [P, GT], F32R)
        q_bd = [sb(f"q_bd{p}", [P, GB, HEADS, P], F32R) for p in range(2)]
        k_bd = sb("k_bd", [P, GB, HEADS, P], F32R)
        k_hi = [sb(f"k_hi{p}", [P, GT], F32R) for p in range(2)]
        k_lo = [sb(f"k_lo{p}", [P, GT], F32R) for p in range(2)]
        V = [sb(f"V{p}", [P, GB, HEADS, HD + 1]) for p in range(2)]
        neg_max = sb("neg_max", [P, P])
        max_t = sb("max_t", [GB * HEADS, P], F32R)
        max_row = sb("max_row", [P, GB, HEADS * P], F32R)
        prob = sb("prob", [P, GB, HEADS, P])
        rsum = sb("rsum", [P, GB, HEADS])
        o = sb("o", [P, GB, P], BF16)
        o_t = sb("o_t", [P, GT], BF16)
        x3 = sb("x3", [P, GB, D])
        x3s = sb("x3s", [P, GB, 2, D], F32R)
        x3t = sb("x3t", [P, GT], F32R)
        xw = sb("xw", [P, GB, D])
        hid = sb("hid", [P, 2, GT])
        wt_rank = sb("wt_rank", [P, P])
        left = sb("left", [P, P])
        top = sb("top", [P, 8])
        over = sb("over", [P, P])
        equal = sb("equal", [P, P])
        order = sb("order", [P, P])
        room = sb("room", [P, 1])
        coef_t = sb("coef_t", [P, P])
        coef = sb("coef", [P, P])

        bank = [ctx.enter_context(nc.psum_tensor(f"bank{n}", [P, 512], F32)) for n in range(8)]

        consts_in = sem("consts_in")
        consts_ready = sem("consts_ready")
        zeros_ready = sem("zeros_ready")
        ids_ready = sem("ids_ready")
        gathered = [sem(f"gathered{p}") for p in range(2)]
        S = {n: sem(n) for n in (
            "idx_ready", "gv_ready", "gt_ready", "vt_ready", "gt_out", "vt_out", "ig_ready", "vi_ready",
            "cat_ready", "catv_ready", "fu_ready", "fused_ready", "ft_ready",
            "st1_ready", "mv1_ready", "rs1_ready", "rm1_ready", "t1_ready",
            "u0_ready", "u_ready", "h1_ready", "st2_ready", "mv2_ready", "rs2_ready", "x2_ready",
            "x2h_ready", "x2s_ready", "xt_ready", "x2t_ready", "q_ready", "k_ready", "v_ready",
            "qm_ready", "qs_ready", "kh_ready", "kl_ready", "v_out", "q_bd_in", "k_bd_in",
            "s_ready", "max_ready", "mt_ready", "max_t_ready", "max_row_in", "st_ready",
            "prob_ready", "pv_ready", "rsum_ready", "o_ready", "ot_ready", "o_t_ready", "wo_ready",
            "h2_ready", "st3_ready", "mv3_ready", "rs3_ready", "x3_ready", "x3h_ready",
            "x3s_ready", "xw_ready", "w_ready", "r_ready", "x3t_ready", "x3t_out", "f1_ready",
            "hid_ready", "f2_ready", "y_ready",
        )}
        wT_ready, topk_step, coefT_ready, cT_ready, coef_ready = (
            sem(n) for n in ("wT_ready", "topk_step", "coefT_ready", "cT_ready", "coef_ready"))
        scaled, summed, pool_scaled, pool_summed = (
            sem(n) for n in ("scaled", "summed", "pool_scaled", "pool_summed"))
        stored = sem("stored")
        passed = sem("passed")

        def wait(eng, name, per, g, k=None, alone=False):
            k = per if k is None else k
            if type(g) is int:
                if g < 0:
                    return
                if g >= NG:
                    g, k = NG - 1, per
            eng.wait_ge(S[name], g * per + k)
            if alone and type(g) is not int:
                eng.sem_inc(passed, 1)

        def on(g):
            return type(g) is not int or 0 <= g < NG

        def of(tile, g):
            return tile[:, bass.ds(g * GB, GB)]

        def pipeline(eng, step, ahead=2):
            turns = (NG - ahead - FIRST) // 2
            for i in range(-2, FIRST):
                step(i, i % 2, i // 2)
            with eng.Fori(0, turns) as t:
                for odd in range(2):
                    step(t * 2 + (FIRST + odd), odd, t + FIRST // 2)
            for i in range(FIRST + 2 * turns, NG + 2):
                step(i, i % 2, i // 2)

        block = ctx.enter_context(nc.Block())

        @block.sync
        def _(sp):
            sp.dma_start(ids_sb[:, :], ids).then_inc(consts_in, 16)
            sp.dma_start(wt[:, :], packed).then_inc(consts_in, 16)
            sp.wait_ge(zeros_ready, 3)

            def step(i, odd, half):
                b, c = i + 1, i
                if on(c):
                    wait(sp, "max_t_ready", 1, c)
                    wait(sp, "st_ready", GB, c - 1)
                    sp.dma_start(max_row[0:1, :, :].rearrange("p b (h q) -> p (b h) q", h=HEADS
                                                              ).bitcast(F32),
                                 max_t[:, :].bitcast(F32)).then_inc(S["max_row_in"], 16)
                if on(b):
                    wait(sp, "kh_ready", 1, b)
                    wait(sp, "s_ready", GB, b - 1)
                    for h in range(HEADS):
                        rows = slice(32 * h, 32 * h + 32)
                        sp.dma_start(k_bd[rows, :, h, :].bitcast(F32),
                                     k_hi[1 - odd][rows, :].rearrange("p (b k) -> p b k", b=GB
                                                                      ).bitcast(F32)
                                     ).then_inc(S["k_bd_in"], 16)
                    wait(sp, "qs_ready", 1, b)
                    wait(sp, "st_ready", GB, b - 2)
                    for h in range(HEADS):
                        rows = slice(32 * h, 32 * h + 32)
                        sp.dma_start(q_bd[1 - odd][rows, :, h, :].bitcast(F32),
                                     q_s[rows, :].rearrange("p (b q) -> p b q", b=GB).bitcast(F32)
                                     ).then_inc(S["q_bd_in"], 16)

            pipeline(sp, step)
            for n in range(P // OC):
                if n % 4 == 3:
                    sp.wait_ge(pool_summed, n // 4 + 1)
                else:
                    sp.wait_ge(summed, n - n // 4 + 1)
                part = slice(n * OC, (n + 1) * OC)
                sp.dma_start(out[part, :, :].rearrange("b t d -> t b d"), R[:, part, :]
                             ).then_inc(stored, 16)
            sp.wait_ge(stored, 16 * (P // OC))

        @block.gpsimd
        def _(pool):
            for p in range(2):
                pool.memset(q_bd[p][:, :, :, :].bitcast(F32), 0.0)
            pool.memset(k_bd[:, :, :, :].bitcast(F32), 0.0)
            pool.memset(max_row[:, :, :].bitcast(F32), 0.0)
            pool.memset(minus_half[:, :], -0.5)
            pool.memset(neg_max[:, :], 0.0)
            pool.memset(o[:, :, :], 0.0).then_inc(zeros_ready, 1)
            pool.wait_ge(zeros_ready, 1)
            pool.memset(o[:, :, D:D + 1], 1.0).then_inc(zeros_ready, 1)
            for p in range(2):
                last = pool.memset(V[p][:, :, :, HD:HD + 1], 1.0)
            last.then_inc(zeros_ready, 1)

            def fetch(g, par):
                pool.tensor_copy(idx[par][:, :], of(idx_all, g)).then_inc(S["idx_ready"], 1)
                wait(pool, "idx_ready", 1, g, alone=True)
                wait(pool, "gt_ready", 1, g - 2, alone=True)
                wait(pool, "gv_ready", 1, g - 2, alone=True)
                wait(pool, "u_ready", 1, g - 2, alone=True)
                for b in range(GB):
                    pool.indirect_dma_start(
                        G[par][:, b, :], None, table,
                        bass.IndirectOffsetOnAxis(ap=idx[par][:, b:b + 1], axis=0),
                    ).then_inc(gathered[par], 16)

            def rstd(mv, rs, src, dst, g):
                wait(pool, src, 1, g, alone=True)
                pool.tensor_scalar(rs[:, :], mv[:, :, 1], LN_EPS, None, ALU.add
                                   ).then_inc(S[dst], 1)
                wait(pool, dst, 2, g, 1, alone=True)
                pool.tensor_tensor(rs[:, :], rs[:, :], minus_half[:, :], ALU.pow
                                   ).then_inc(S[dst], 1)

            def visit(g, par, g_half):
                pool.wait_ge(gathered[par], g_half * 64 + 64)
                wait(pool, "vt_ready", 1, g - 1, alone=True)
                pool.tensor_copy(gv[:, :, :], G[par][:, :, 2 * D:FEAT]).then_inc(S["gv_ready"], 1)

            pool.wait_ge(ids_ready, 2)
            pool.wait_ge(consts_ready, 1)
            pool.wait_ge(zeros_ready, 3)
            fetch(0, 0)
            visit(0, 0, 0)

            def step(i, odd, half):
                a, d, nxt = i + 2, i - 2, i + 3
                if on(d):
                    rstd(mv3, rs3, "mv3_ready", "rs3_ready", d)
                if on(nxt):
                    fetch(nxt, 1 - odd)
                if on(d):
                    wait(pool, "x3_ready", 1, d, alone=True)
                    wait(pool, "w_ready", 1, d - 1, alone=True)
                    pool.tensor_tensor(xw[:, :, :], x3[:, :, :],
                                       w["wr"].unsqueeze(1).to_broadcast([P, GB, D]), ALU.mult
                                       ).then_inc(S["xw_ready"], 1)
                    pool.tensor_tensor(of(R, d), of(R, d), x3[:, :, :], ALU.add
                                       ).then_inc(S["r_ready"], 1)
                if on(a):
                    wait(pool, "h1_ready", 1, a - 1, alone=True)
                    pool.tensor_tensor(
                        u0[:, :, :], of(valid, a).unsqueeze(2).to_broadcast([P, GB, D]),
                        b_tenth[:, :].unsqueeze(1).to_broadcast([P, GB, D]), ALU.mult
                    ).then_inc(S["u0_ready"], 1)
                    wait(pool, "u0_ready", 1, a, alone=True)
                    pool.tensor_tensor(u[:, :, :], u0[:, :, :], G[odd][:, :, 0:D], ALU.add
                                       ).then_inc(S["u_ready"], 1)
                    rstd(mv1, rs1, "mv1_ready", "rs1_ready", a)
                    wait(pool, "rs1_ready", 2, a, alone=True)
                    pool.tensor_tensor(rs1[:, :], rs1[:, :], of(valid, a), ALU.mult
                                       ).then_inc(S["rm1_ready"], 1)
                if on(nxt):
                    visit(nxt, 1 - odd, half + 1 + odd)
                if on(a):
                    rstd(mv2, rs2, "mv2_ready", "rs2_ready", a)

            pipeline(pool, step, ahead=3)
            pool.wait_ge(coef_ready, 1)
            wait(pool, "y_ready", 1, NG - 1, alone=True)
            wait(pool, "r_ready", 1, NG - 1, alone=True)
            for m, n in enumerate(range(3, P // OC, 4)):
                part = slice(n * OC, (n + 1) * OC)
                pool.tensor_tensor(Y[:, part, :], Y[:, part, :],
                                   coef[:, part].unsqueeze(2).to_broadcast([P, OC, D]), ALU.mult
                                   ).then_inc(pool_scaled, 1)
                pool.wait_ge(pool_scaled, m + 1)
                pool.tensor_tensor(R[:, part, :], R[:, part, :], Y[:, part, :], ALU.add
                                   ).then_inc(pool_summed, 1)

        @block.scalar
        def _(act):
            act.wait_ge(consts_ready, 1)
            act.wait_ge(zeros_ready, 3)

            def step(i, odd, half):
                a, b, c, e, d = i + 2, i + 1, i, i - 1, i - 2
                if on(a):
                    wait(act, "gt_ready", 1, a)
                    act.activation(ig_in[:, :], bank[4][:, :], ACT.Copy).then_inc(S["gt_out"], 1)
                    wait(act, "vt_ready", 1, a)
                    act.activation(vi_in[0:GB * VD, :], bank[5][0:GB * VD, 0:P], ACT.Copy
                                   ).then_inc(S["vt_out"], 1)
                    wait(act, "ig_ready", 1, a)
                    act.activation(cat[:, :], bank[6][:, :], ACT.Gelu, bias=w["b_ig"]
                                   ).then_inc(S["cat_ready"], 1)
                    wait(act, "vi_ready", 1, a)
                    act.activation(catv[:, :], bank[7][:, 0:2 * P], ACT.Gelu, bias=w["b_vi"]
                                   ).then_inc(S["catv_ready"], 1)
                if on(c):
                    wait(act, "mt_ready", 1, c)
                    wait(act, "max_row_in", 16, c - 1)
                    act.activation(max_t[:, :], bank[0][0:GB * HEADS, 0:P], ACT.Copy
                                   ).then_inc(S["max_t_ready"], 1)
                if on(a):
                    wait(act, "fu_ready", 1, a)
                    wait(act, "ft_ready", 1, a - 1)
                    act.activation(fused[:, :], bank[6][:, 0:2 * P], ACT.Gelu, bias=w["b_fu"]
                                   ).then_inc(S["fused_ready"], 1)
                if on(b):
                    wait(act, "xt_ready", 1, b)
                    wait(act, "v_ready", 1, b - 1)
                    act.activation(x2t[:, :], bank[4][:, :], ACT.Copy).then_inc(S["x2t_ready"], 1)
                if on(d):
                    wait(act, "x3t_ready", 1, d)
                    act.activation(x3t[:, :], bank[7][:, :], ACT.Copy).then_inc(S["x3t_out"], 1)
                if on(b):
                    wait(act, "q_ready", 1, b)
                    wait(act, "qs_ready", 1, b - 1)
                    act.activation(q_mask[:, :].bitcast(F32R), bank[4][:, :], ACT.Identity,
                                   bias=bq_lo[:, :], scale=w["lo_row"]).then_inc(S["qm_ready"], 1)
                    wait(act, "k_ready", 1, b)
                    wait(act, "st_ready", GB, b - 2)
                    wait(act, "k_bd_in", 64, b - 2)
                    act.activation(k_hi[1 - odd][:, :], bank[3][:, :], ACT.Identity,
                                   bias=w["b_k"]).then_inc(S["kh_ready"], 1)
                if on(d):
                    wait(act, "f2_ready", 1, d - 1)
                    for m in range(2):
                        wait(act, "f1_ready", 2, d, m + 1)
                        act.activation(hid[:, m, :], bank[7 - m][:, :], ACT.Gelu_apprx_tanh,
                                       bias=w["b_1"][:, m:m + 1]).then_inc(S["hid_ready"], 1)
                for s in range(GB):
                    if on(c):
                        wait(act, "pv_ready", 1, c - 1)
                        wait(act, "st_ready", GB, c, s + 1)
                        act.activation(prob[:, s, :, :].rearrange("p h q -> p (h q)"),
                                       bank[s][:, :], ACT.Exp, scale=SCALE
                                       ).then_inc(S["prob_ready"], 1)
                    if s == 1 and on(e):
                        wait(act, "ot_ready", 1, e)
                        wait(act, "wo_ready", 1, e - 1)
                        act.activation(o_t[:, :], bank[5][:, 0:GT // 2].bitcast(BF16), ACT.Copy
                                       ).then_inc(S["o_t_ready"], 1)

            pipeline(act, step)

        @block.vector
        def _(dve):
            dve.wait_ge(consts_in, 32)
            dve.tensor_scalar(idx_all[:, :], ids_sb[:, :], 0, 25000, ALU.max, ALU.min
                              ).then_inc(ids_ready, 1)
            dve.tensor_scalar(valid[:, :], ids_sb[:, :], 0, None, ALU.not_equal
                              ).then_inc(ids_ready, 1)
            dve.memset(ones_r[:, :].bitcast(F32), 1.0)
            dve.tensor_copy(w_hi[:, :], wt[:, 0:SPLIT])
            dve.tensor_copy(wo_part[:, 0, :], w["w_o"])
            dve.tensor_copy(ident_bf[:, :], ident)
            dve.tensor_scalar(g_tenth[:, :], w["gamma"], 0.1, None, ALU.mult)
            dve.tensor_scalar(b_tenth[:, :], w["beta"], 0.1, None, ALU.mult)
            dve.tensor_tensor(bq_lo[:, :], w["b_q"], w["lo_row"], ALU.mult).then_inc(topk_step, 1)
            dve.wait_ge(topk_step, 1)
            dve.tensor_tensor(w_lo[:, :], wt[:, 0:SPLIT], w_hi[:, :].bitcast(F32), ALU.subtract)
            dve.tensor_tensor(wo_rest[:, 0, :], w["w_o"], wo_part[:, 0, :], ALU.subtract
                              ).then_inc(topk_step, 1)
            dve.wait_ge(topk_step, 2)
            dve.tensor_copy(wo_part[:, 1, :], wo_rest[:, 0, :]).then_inc(topk_step, 1)
            dve.wait_ge(topk_step, 3)
            dve.tensor_tensor(wo_rest[:, 1, :], wo_rest[:, 0, :], wo_part[:, 1, :], ALU.subtract
                              ).then_inc(topk_step, 1)
            dve.wait_ge(topk_step, 4)
            dve.tensor_copy(wo_part[:, 2, :], wo_rest[:, 1, :]).then_inc(consts_ready, 1)
            setup_steps = 4
            dve.wait_ge(consts_ready, 1)
            dve.wait_ge(zeros_ready, 3)

            def stats(src, st, mv, st_done, mv_done, g):
                for b in range(GB):
                    last = dve.bn_stats(st[:, b, :], src(b))
                last.then_inc(S[st_done], 1)
                wait(dve, st_done, 1, g, alone=True)
                for b in range(GB):
                    last = dve.bn_aggr(mv[:, b, :], st[:, b, :])
                last.then_inc(S[mv_done], 1)

            def normalize(dst, src, mv, rs, done, g):
                for b in range(GB):
                    last = dve.tensor_scalar(dst[:, b, :], src(b), mv[:, b, 0:1], rs[:, b:b + 1],
                                             ALU.subtract, ALU.mult)
                last.then_inc(S[done], 1)

            def split(dst, src, hi_done, lo_done, g):
                dve.tensor_copy(dst[:, :, 0, :], src[:, :, :]).then_inc(S[hi_done], 1)
                wait(dve, hi_done, 1, g)
                dve.tensor_tensor(dst[:, :, 1, :], src[:, :, :], dst[:, :, 0, :].bitcast(F32),
                                  ALU.subtract).then_inc(S[lo_done], 1)

            def kept(g):
                return lambda s: R[:, bass.ds(g * GB + s, 1), :].rearrange("p b d -> p (b d)")

            ft = bank[5][:, 0:GB * D].rearrange("p (b d) -> p b d", b=GB)

            n = [setup_steps]

            def done(ins):
                n[0] += 1
                ins.then_inc(topk_step, 1)
                dve.wait_ge(topk_step, n[0])

            def select():
                dve.wait_ge(wT_ready, 1)
                done(dve.tensor_scalar(wt_rank[:, :], bank[0][:, 0:P], w["br"], None, ALU.add))
                done(dve.tensor_copy(left[:, :], wt_rank[:, :]))
                for _ in range(KEEP // 8):
                    done(dve.max(top[:, :], left[:, :]))
                    done(dve.match_replace(left[:, :], top[:, :], left[:, :], LOWEST))
                done(dve.max(top[:, :], left[:, :]))
                least = top[:, KEEP % 8 - 1:KEEP % 8]
                done(dve.tensor_scalar(over[:, :], wt_rank[:, :], least, None, ALU.is_gt))
                done(dve.tensor_scalar(equal[:, :], wt_rank[:, :], least, None, ALU.is_equal))
                done(dve.tensor_tensor_scan(order[:, :], ones_r[:, :].bitcast(F32), equal[:, :], 0.0,
                                            ALU.mult, ALU.add))
                done(dve.tensor_reduce(room[:, :], over[:, :], AX, ALU.add, negate=True))
                done(dve.tensor_scalar(room[:, :], room[:, :], float(KEEP), None, ALU.add))
                done(dve.scalar_tensor_tensor(order[:, :], order[:, :], room[:, :], equal[:, :],
                                              ALU.is_le, ALU.mult))
                done(dve.tensor_tensor(order[:, :], order[:, :], over[:, :], ALU.add))
                dve.tensor_tensor(coef_t[:, :], order[:, :], wt_rank[:, :], ALU.mult
                                  ).then_inc(coefT_ready, 1)

            def step(i, odd, half):
                a, b, c, e, d = i + 2, i + 1, i, i - 1, i - 2
                if on(d):
                    wait(dve, "wo_ready", 1, d)
                    dve.tensor_tensor(of(R, d), of(R, d),
                                      bank[6][:, 0:GB * D].rearrange("p (b d) -> p b d", b=GB),
                                      ALU.add).then_inc(S["h2_ready"], 1)
                    wait(dve, "h2_ready", 1, d, alone=True)
                    stats(kept(d), st3, mv3, "st3_ready", "mv3_ready", d)
                if on(c):
                    for s in range(GB):
                        wait(dve, "s_ready", GB, c, s + 1)
                        dve.tensor_reduce(neg_max[:, HEADS * s:HEADS * s + HEADS],
                                          bank[s][:, :].rearrange("p (h k) -> p h k", h=HEADS),
                                          AX, ALU.max, negate=True).then_inc(S["max_ready"], 1)
                if on(b):
                    wait(dve, "rs2_ready", 2, b)
                    normalize(x2, kept(b), mv2, rs2, "x2_ready", b)
                    wait(dve, "x2_ready", 1, b)
                    wait(dve, "xt_ready", 1, b - 1)
                    split(x2s, x2, "x2h_ready", "x2s_ready", b)
                if on(d):
                    wait(dve, "rs3_ready", 2, d)
                    wait(dve, "r_ready", 1, d - 1)
                    normalize(x3, kept(d), mv3, rs3, "x3_ready", d)
                    wait(dve, "x3_ready", 1, d)
                    wait(dve, "x3t_ready", 1, d - 1)
                    split(x3s, x3, "x3h_ready", "x3s_ready", d)
                if on(e):
                    pv = bank[5][:, 0:GB * HEADS * (HD + 1)].rearrange(
                        "p (b h d) -> p b h d", b=GB, h=HEADS)
                    wait(dve, "pv_ready", 1, e)
                    dve.reciprocal(rsum[:, :, :], pv[:, :, :, HD]).then_inc(S["rsum_ready"], 1)
                    wait(dve, "rsum_ready", 1, e)
                    wait(dve, "ot_ready", 1, e - 1)
                    dve.tensor_tensor(
                        o[:, :, 0:D].rearrange("p b (h d) -> p b h d", h=HEADS), pv[:, :, :, 0:HD],
                        rsum[:, :, :].unsqueeze(3).to_broadcast([P, GB, HEADS, HD]), ALU.mult
                    ).then_inc(S["o_ready"], 1)
                if on(b):
                    wait(dve, "qm_ready", 1, b)
                    wait(dve, "q_bd_in", 64, b - 1)
                    wait(dve, "s_ready", GB, b - 1)
                    dve.scalar_tensor_tensor(q_s[:, :], bank[4][:, :], w["b_q"], q_mask[:, :],
                                             ALU.add, ALU.subtract).then_inc(S["qs_ready"], 1)
                    wait(dve, "kh_ready", 1, b)
                    wait(dve, "st_ready", GB, b - 2)
                    dve.scalar_tensor_tensor(k_lo[1 - odd][:, :], bank[3][:, :], w["b_k"],
                                             k_hi[1 - odd][:, :].bitcast(F32),
                                             ALU.add, ALU.subtract).then_inc(S["kl_ready"], 1)
                if on(a):
                    wait(dve, "ft_ready", 1, a, alone=True)
                    stats(lambda s: ft[:, s, :], st1, mv1, "st1_ready", "mv1_ready", a)
                    wait(dve, "mv1_ready", 1, a)
                    for s in range(GB):
                        last = dve.scalar_tensor_tensor(t1[:, s, :], ft[:, s, :], mv1[:, s, 0:1],
                                                        g_tenth[:, :], ALU.subtract, ALU.mult)
                    last.then_inc(S["t1_ready"], 1)
                if on(b):
                    wait(dve, "v_ready", 1, b)
                    wait(dve, "pv_ready", 1, b - 2)
                    dve.tensor_tensor(
                        V[1 - odd][:, :, :, 0:HD],
                        bank[4][:, 0:GB * D].rearrange("p (b h d) -> p b h d", b=GB, h=HEADS),
                        w["bv"].rearrange("p (h d) -> p h d", h=HEADS).unsqueeze(1).to_broadcast(
                            [P, GB, HEADS, HD]), ALU.add).then_inc(S["v_out"], 1)
                if on(d):
                    wait(dve, "xw_ready", 1, d)
                    dve.tensor_reduce(of(W, d), xw[:, :, :], AX, ALU.add
                                      ).then_inc(S["w_ready"], 1)
                if on(a):
                    wait(dve, "t1_ready", 1, a)
                    wait(dve, "u_ready", 1, a)
                    wait(dve, "rm1_ready", 1, a)
                    for s in range(GB):
                        last = dve.scalar_tensor_tensor(kept(a)(s), t1[:, s, :], rs1[:, s:s + 1],
                                                        u[:, s, :], ALU.mult, ALU.add)
                    last.then_inc(S["h1_ready"], 1)
                    wait(dve, "h1_ready", 1, a, alone=True)
                    stats(kept(a), st2, mv2, "st2_ready", "mv2_ready", a)
                if type(d) is int and d == NG - 1:
                    select()
                if on(d):
                    wait(dve, "f2_ready", 1, d)
                    dve.tensor_tensor(
                        of(Y, d), bank[7][:, 0:GB * D].rearrange("p (b d) -> p b d", b=GB),
                        w["b2"].unsqueeze(1).to_broadcast([P, GB, D]), ALU.add
                    ).then_inc(S["y_ready"], 1)

            pipeline(dve, step)

            dve.wait_ge(cT_ready, 1)
            dve.tensor_copy(coef[:, :], bank[1][:, 0:P]).then_inc(coef_ready, 1)
            dve.wait_ge(coef_ready, 1)
            wait(dve, "r_ready", 1, NG - 1)
            m = 0
            for k in range(P // OC):
                if k % 4 == 3:
                    continue
                part = slice(k * OC, (k + 1) * OC)
                dve.tensor_tensor(Y[:, part, :], Y[:, part, :],
                                  coef[:, part].unsqueeze(2).to_broadcast([P, OC, D]), ALU.mult
                                  ).then_inc(scaled, 1)
                m += 1
                dve.wait_ge(scaled, m)
                dve.tensor_tensor(R[:, part, :], R[:, part, :], Y[:, part, :], ALU.add
                                  ).then_inc(summed, 1)

        @block.tensor
        def _(pe):
            pe.wait_ge(consts_ready, 1)
            pe.wait_ge(zeros_ready, 3)
            mm = nc.tensor.matmul

            def values(e, odd, seqs):
                for s in seqs:
                    for h in range(HEADS):
                        at = (s * HEADS + h) * (HD + 1)
                        last = mm(bank[5][:, at:at + HD + 1], prob[:, s, h, :],
                                  V[1 - odd][:, s, h, :], start=True, stop=True)
                return last

            def scores_t(c, odd, seqs):
                for s in seqs:
                    tok = slice(s * P, (s + 1) * P)
                    q = q_bd[odd][:, s, :, :].rearrange("p h q -> p (h q)")
                    mm(bank[s][:, :], k_hi[odd][:, tok], q, start=True, stop=False)
                    mm(bank[s][:, :], k_lo[odd][:, tok], q, start=False, stop=False)
                    mm(bank[s][:, :], ones_r[:, :], max_row[:, s, :], start=False, stop=True
                       ).then_inc(S["st_ready"], 1)

            def step(i, odd, half):
                a, b, c, e, d = i + 2, i + 1, i, i - 1, i - 2
                if on(a):
                    pe.wait_ge(gathered[odd], (half + 1) * 64 + 64)
                    wait(pe, "v_out", 1, a - 2)
                    for s in range(GB):
                        last = mm(bank[4][:, s * P:(s + 1) * P], G[odd][:, s, 0:2 * D], ident,
                                  start=True, stop=True, is_transpose=True)
                    last.then_inc(S["gt_ready"], 1)
                if on(a):
                    wait(pe, "gv_ready", 1, a)
                    wait(pe, "t1_ready", 1, a - 1)
                    wait(pe, "o_t_ready", 1, a - 4)
                    mm(bank[5][0:GB * VD, 0:P], gv[:, :, :].rearrange("p b d -> p (b d)"), ident,
                       start=True, stop=True, is_transpose=True).then_inc(S["vt_ready"], 1)
                if on(c):
                    wait(pe, "k_bd_in", 64, c)
                    wait(pe, "qs_ready", 1, c)
                    for s in range(GB):
                        wait(pe, "prob_ready", GB, c - 1, s + 1)
                        mm(bank[s][:, :], q_s[:, s * P:(s + 1) * P],
                           k_bd[:, s, :, :].rearrange("p h k -> p (h k)"), start=True, stop=True
                           ).then_inc(S["s_ready"], 1)
                if on(a):
                    wait(pe, "gt_out", 1, a)
                    wait(pe, "h2_ready", 1, a - 4)
                    mm(bank[6][:, :], w["w_ig"], ig_in[:, :], start=True, stop=True
                       ).then_inc(S["ig_ready"], 1)
                if on(e):
                    wait(pe, "prob_ready", GB, e)
                    wait(pe, "v_out", 1, e)
                    wait(pe, "vt_out", 1, e + 3)
                    values(e, odd, (0,))
                if on(a):
                    wait(pe, "vt_out", 1, a)
                    wait(pe, "y_ready", 1, a - 5)
                    for n in range(2):
                        last = mm(bank[7][:, n * P:(n + 1) * P],
                                  w["w_vi"][0:GB * VD, n * P:(n + 1) * P], vi_in[0:GB * VD, :],
                                  start=True, stop=True)
                    last.then_inc(S["vi_ready"], 1)
                if on(e):
                    values(e, odd, (1,))
                if on(c):
                    wait(pe, "max_ready", GB, c)
                    mm(bank[0][:, 0:P], neg_max[:, :], ident, start=True, stop=True,
                       is_transpose=True).then_inc(S["mt_ready"], 1)
                if on(a):
                    wait(pe, "catv_ready", 1, a)
                    mm(bank[6][:, 0:2 * P], w["w_fv"], catv[:, :], start=True, stop=False)
                    for n, wf in enumerate(("w_fe", "w_fo")):
                        last = mm(bank[6][:, 0:2 * P], w[wf],
                                  cat[:, :].rearrange("p (r s q) -> p s r q", r=2, s=2)[:, n],
                                  start=False, stop=(n == 1))
                    last.then_inc(S["fu_ready"], 1)
                if on(e):
                    values(e, odd, (2,))
                if on(b):
                    wait(pe, "x2s_ready", 1, b)
                    wait(pe, "gt_out", 1, b + 1)
                    for s in range(GB):
                        last = mm(bank[4][:, s * P:(s + 1) * P],
                                  x2s[:, s, :, :].rearrange("p k d -> p (k d)").bitcast(F32),
                                  ident, start=True, stop=True, is_transpose=True)
                    last.then_inc(S["xt_ready"], 1)
                if on(e):
                    values(e, odd, (3,)).then_inc(S["pv_ready"], 1)
                if on(d):
                    wait(pe, "x3s_ready", 1, d)
                    wait(pe, "catv_ready", 1, d + 4)
                    for s in range(GB):
                        last = mm(bank[7][:, s * P:(s + 1) * P],
                                  x3s[:, s, :, :].rearrange("p k d -> p (k d)").bitcast(F32),
                                  ident, start=True, stop=True, is_transpose=True)
                    last.then_inc(S["x3t_ready"], 1)
                if on(b):
                    wait(pe, "x2t_ready", 1, b)
                    mm(bank[4][:, :], hi["w_q"], x2t[:, :], start=True, stop=False)
                    mm(bank[4][:, :], lo["w_q"], x2t[:, :], start=False, stop=True
                       ).then_inc(S["q_ready"], 1)
                if on(b):
                    wait(pe, "max_ready", GB, b - 1)
                    mm(bank[3][:, :], hi["w_k"], x2t[:, :], start=True, stop=False)
                    mm(bank[3][:, :], lo["w_k"], x2t[:, :], start=False, stop=True
                       ).then_inc(S["k_ready"], 1)
                if on(d):
                    wait(pe, "x3t_out", 1, d)
                    wait(pe, "fused_ready", 1, d + 4)
                    for m in range(2):
                        cols = slice(m * P, (m + 1) * P)
                        mm(bank[7 - m][:, :], hi["w_1"][:, cols], x3t[:, :], start=True, stop=False)
                        mm(bank[7 - m][:, :], lo["w_1"][:, cols], x3t[:, :], start=False, stop=True
                           ).then_inc(S["f1_ready"], 1)
                if type(d) is int and d == NG - 1:
                    wait(pe, "w_ready", 1, d)
                    mm(bank[0][:, 0:P], W[:, :], ident, start=True, stop=True, is_transpose=True
                       ).then_inc(wT_ready, 1)
                if on(a):
                    wait(pe, "fused_ready", 1, a)
                    wait(pe, "o_ready", 1, a - 3)
                    for n in range(2):
                        last = mm(bank[5][:, n * P:(n + 1) * P], fused[:, n * P:(n + 1) * P],
                                  ident, start=True, stop=True, is_transpose=True)
                    last.then_inc(S["ft_ready"], 1)
                if on(c):
                    wait(pe, "max_row_in", 16, c)
                    wait(pe, "q_bd_in", 64, c)
                    scores_t(c, odd, (0,))
                if on(b):
                    wait(pe, "qs_ready", 1, b)
                    for s in range(GB):
                        xs = x2t[:, s * P:(s + 1) * P]
                        mm(bank[4][:, s * D:(s + 1) * D], xs, hi["w_v"], start=True, stop=False)
                        last = mm(bank[4][:, s * D:(s + 1) * D], xs, lo["w_v"],
                                  start=False, stop=True)
                    last.then_inc(S["v_ready"], 1)
                if on(c):
                    scores_t(c, odd, (1, 2))
                    wait(pe, "kl_ready", 1, c + 1)
                    scores_t(c, odd, (3,))
                if on(e):
                    wait(pe, "o_ready", 1, e)
                    wait(pe, "t1_ready", 1, e + 3)
                    for s in range(GB):
                        last = mm(bank[5][:, s * P // 2:(s + 1) * P // 2].bitcast(BF16),
                                  o[:, s, :], ident_bf[:, :], start=True, stop=True,
                                  is_transpose=True)
                    last.then_inc(S["ot_ready"], 1)
                if on(d):
                    wait(pe, "hid_ready", 2, d)
                    for s in range(GB):
                        for m in range(2):
                            last = mm(bank[7][:, s * D:(s + 1) * D], hid[:, m, s * P:(s + 1) * P],
                                      w["w_2"][:, m * D:(m + 1) * D], start=(m == 0), stop=(m == 1))
                    last.then_inc(S["f2_ready"], 1)
                if on(e):
                    wait(pe, "o_t_ready", 1, e)
                    wait(pe, "hid_ready", 2, e - 1)
                    for s in range(GB):
                        for n in range(3):
                            last = mm(bank[6][:, s * D:(s + 1) * D],
                                      o_t[0:D + 1, s * P:(s + 1) * P], wo_part[0:D + 1, n, :],
                                      start=(n == 0), stop=(n == 2))
                    last.then_inc(S["wo_ready"], 1)

            pipeline(pe, step)
            pe.wait_ge(coefT_ready, 1)
            mm(bank[1][:, 0:P], coef_t[:, :], ident, start=True, stop=True, is_transpose=True
               ).then_inc(cT_ready, 1)


def kernel(x, L0_tok_emb_table, L0_tok_geo_table, L0_tok_visit_table, L0_tok_w_item,
           L0_tok_b_item, L0_tok_w_geo, L0_tok_b_geo, L0_tok_w_visit, L0_tok_b_visit,
           L0_tok_w_fuse, L0_tok_b_fuse, L0_tok_ln_gamma, L0_tok_ln_beta, L0_attn_Wq, L0_attn_bq,
           L0_attn_Wk, L0_attn_bk, L0_attn_Wv, L0_attn_bv, L0_attn_Wo, L0_attn_bo,
           L0_ffn_attention_mask, L0_ffn_wr, L0_ffn_br, L0_ffn_w1, L0_ffn_b1, L0_ffn_w2,
           L0_ffn_b2):
    import numpy as np
    import concourse.bacc as bacc
    from concourse.bass_utils import run_bass_kernel_spmd

    c = {n: np.zeros((P, b - a), np.float32) for n, (a, b) in COL.items()}

    def per_head(wt):
        wt = wt.reshape(wt.shape[0], HEADS, 1, HD)
        return np.broadcast_to(wt, (wt.shape[0], HEADS, 2, HD)).reshape(wt.shape[0], P)

    for n, src in (("w_q", L0_attn_Wq), ("w_k", L0_attn_Wk)):
        c[n][:D] = c[n][D:] = per_head(np.asarray(src).T)
    c["w_v"][:D] = c["w_v"][D:] = np.asarray(L0_attn_Wv).T
    c["w_1"][:D] = c["w_1"][D:] = np.asarray(L0_ffn_w1)
    c["w_ig"][:D, :D] = np.asarray(L0_tok_w_item)
    c["w_ig"][D:, D:] = np.asarray(L0_tok_w_geo)
    for s in range(GB):
        at = (s // 2) * P + (s % 2) * D
        c["w_vi"][s * VD:(s + 1) * VD, at:at + D] = np.asarray(L0_tok_w_visit)
    wf = np.asarray(L0_tok_w_fuse)
    c["w_fe"][:, :D] = c["w_fo"][:, D:] = wf[:P]
    c["w_fv"][:D, :D] = c["w_fv"][D:, D:] = wf[P:]
    c["w_2"][:, :D], c["w_2"][:, D:] = np.asarray(L0_ffn_w2)[:P], np.asarray(L0_ffn_w2)[P:]
    c["w_o"][:D], c["w_o"][D] = np.asarray(L0_attn_Wo).T, np.asarray(L0_attn_bo)
    c["ident"][:] = np.eye(P, dtype=np.float32)
    for n, src in (("gamma", L0_tok_ln_gamma), ("beta", L0_tok_ln_beta), ("bv", L0_attn_bv),
                   ("b2", L0_ffn_b2), ("wr", L0_ffn_wr), ("br", L0_ffn_br)):
        c[n][:] = np.asarray(src).reshape(1, -1)
    c["b_ig"][:D, 0], c["b_ig"][D:, 0] = np.asarray(L0_tok_b_item), np.asarray(L0_tok_b_geo)
    for n, src in (("b_vi", L0_tok_b_visit), ("b_fu", L0_tok_b_fuse)):
        c[n][:D, 0] = c[n][D:, 0] = np.asarray(src)
    for n, src in (("b_q", L0_attn_bq), ("b_k", L0_attn_bk)):
        c[n][:, 0] = per_head(np.asarray(src).reshape(1, D))[0]
    c["b_1"][:, 0], c["b_1"][:, 1] = np.asarray(L0_ffn_b1)[:P], np.asarray(L0_ffn_b1)[P:]
    c["lo_row"][:, 0] = np.arange(P) // HD % 2

    arrays = {
        "ids": np.ascontiguousarray(np.asarray(x).T),
        "table": np.concatenate([np.asarray(L0_tok_emb_table), np.asarray(L0_tok_geo_table),
                                 np.asarray(L0_tok_visit_table)], axis=1),
        "packed": np.concatenate([c[n] for n, _ in _COLS], axis=1),
    }
    nc = bacc.Bacc("TRN2", target_bir_lowering=False, num_devices=1)
    args = [nc.dram_tensor(n, a.shape, mybir.dt.from_np(a.dtype), kind="ExternalInput").ap()
            for n, a in arrays.items()]
    out = nc.dram_tensor("out", (P, P, D), F32, kind="ExternalOutput").ap()
    build(nc, *args, out)
    r = run_bass_kernel_spmd(nc, [arrays], core_ids=[0])
    return r.results[0]["out"]
```

```python
from contextlib import ExitStack

import concourse.bass as bass
from concourse import mybir

F32 = mybir.dt.float32
F32R = mybir.dt.float32r
BF16 = mybir.dt.bfloat16
I32 = mybir.dt.int32
ALU = mybir.AluOpType
ACT = mybir.ActivationFunctionType
AX = mybir.AxisListType.X

P = 128
D = 64
VD = 24
FEAT = 2 * D + VD
HEADS = 4
HD = D // HEADS
HID = 4 * D
GB = 4
NG = P // GB
GT = GB * P
KEEP = P // 2 - 1
LN_EPS = 1e-5
SCALE = HD ** -0.5
LOWEST = -3.0e38
FIRST = 4
TAIL = P - GB * 4
PARTS = ((0, TAIL), (TAIL, P))
DVE_SUMS = ((0, 16), (16, 8), (24, 16), (40, 8), (48, 8), (56, 8), (TAIL, 8), (P - GB, GB))
POOL_SUMS = ((64, 8), (72, 8), (80, 8), (88, 8), (96, 8), (104, 8), (TAIL + 8, 4))
ACT_SCALES = (2, 5)
STORES = "DPDDPDDPPPDPDPD"
SPLIT_ROUNDS = 4

_COLS = [
    ("w_q", P), ("w_k", P), ("w_v", D), ("w_1", HID),
    ("w_ig", P), ("w_vi", 2 * P), ("w_fe", P), ("w_fo", P), ("w_fv", P), ("w_2", 2 * D),
    ("w_o", D), ("ident", P),
    ("gamma", D), ("beta", D), ("bv", D), ("b2", D), ("wr", D), ("br", 1),
    ("b_ig", 1), ("b_vi", 1), ("b_fu", 1), ("b_q", 1), ("b_k", 1), ("b_1", 2), ("lo_row", 1),
]
COL, _at = {}, 0
for _n, _c in _COLS:
    COL[_n] = (_at, _at + _c)
    _at += _c
PACKED = _at
SPLIT = COL["w_1"][1]


def build(nc, ids, table, packed, out):
    with ExitStack() as ctx:
        def sb(name, shape, dt=F32):
            return ctx.enter_context(nc.sbuf_tensor(name, shape, dt))

        def sem(name):
            return ctx.enter_context(nc.semaphore(name))

        wt = sb("wt", [P, PACKED])
        w = {n: wt[:, a:b] for n, (a, b) in COL.items()}
        w_hi = sb("w_hi", [P, SPLIT], F32R)
        w_lo = sb("w_lo", [P, SPLIT], F32R)
        hi = {n: w_hi[:, COL[n][0]:COL[n][1]] for n in ("w_q", "w_k", "w_1")}
        lo = {n: w_lo[:, COL[n][0]:COL[n][1]] for n in ("w_q", "w_k", "w_1")}
        v_parts = sb("v_parts", [P, 2, D], F32R)
        wo_part = sb("wo_part", [P, 3, D], BF16)
        wo_rest = sb("wo_rest", [P, 2, D])
        ident = w["ident"]
        ident_bf = sb("ident_bf", [P, P], BF16)
        ones_r = sb("ones_r", [P, P], F32R)
        g_tenth = sb("g_tenth", [P, D])
        b_tenth = sb("b_tenth", [P, D])
        bq_lo = sb("bq_lo", [P, 1])
        ids_sb = sb("ids_sb", [P, P], I32)
        idx_all = sb("idx_all", [P, P], I32)
        valid = sb("valid", [P, P])

        R = sb("R", [P, P, D])
        Y = sb("Y", [P, P, D])
        W = sb("W", [P, P])

        idx = [sb(f"idx{p}", [P, GB], I32) for p in range(2)]
        G = [sb(f"G{p}", [P, GB, FEAT]) for p in range(2)]
        gv = sb("gv", [P, GB, VD])
        ig_in = sb("ig_in", [P, GT])
        vi_in = sb("vi_in", [P, P])
        cat = sb("cat", [P, GT])
        catv = sb("catv", [P, 2 * P])
        fused = sb("fused", [P, 2 * P])
        st1, st2, st3 = (sb(f"st{n}", [P, GB, 6]) for n in (1, 2, 3))
        mv1, mv2, mv3 = (sb(f"mv{n}", [P, GB, 2]) for n in (1, 2, 3))
        rs1, rs2, rs3 = (sb(f"rs{n}", [P, GB]) for n in (1, 2, 3))
        minus_half = sb("minus_half", [P, GB])
        t1 = sb("t1", [P, GB, D])
        u = sb("u", [P, GB, D])
        u0 = sb("u0", [P, GB, D])
        x2 = sb("x2", [P, GB, D])
        x2s = sb("x2s", [P, GB, 2, D], F32R)
        x2t = sb("x2t", [P, GT], F32R)
        q_mask = sb("q_mask", [P, GT])
        q_s = sb("q_s", [P, GT], F32R)
        q_bd = [sb(f"q_bd{p}", [P, GB, 2, 2, P], F32R) for p in range(2)]
        k_pair = [sb(f"k_pair{p}", [P, 2, GT], F32R) for p in range(2)]
        k_bd = sb("k_bd", [P, GB, HEADS, P], F32R)
        k_hi = [sb(f"k_hi{p}", [P, GT], F32R) for p in range(2)]
        k_lo = [sb(f"k_lo{p}", [P, GT], F32R) for p in range(2)]
        V = [sb(f"V{p}", [P, GB, HEADS, HD + 1]) for p in range(2)]
        neg_max = sb("neg_max", [P, P])
        max_t = sb("max_t", [GB * HEADS, P], F32R)
        max_row = sb("max_row", [P, GB, HEADS * P], F32R)
        prob = sb("prob", [P, GB, HEADS, P])
        rsum = sb("rsum", [P, GB, HEADS])
        o = sb("o", [P, GB, P], BF16)
        o_t = sb("o_t", [P, GT], BF16)
        x3 = sb("x3", [P, GB, D])
        x3s = sb("x3s", [P, GB, 2, D], F32R)
        x3t = sb("x3t", [P, GT], F32R)
        xw = sb("xw", [P, GB, D])
        hid = sb("hid", [P, 2, GT])
        wt_rank = sb("wt_rank", [P, P])
        left = sb("left", [P, P])
        top = sb("top", [P, 8])
        over = sb("over", [P, P])
        equal = sb("equal", [P, P])
        order = sb("order", [P, P])
        room = sb("room", [P, 1])
        coef_t = sb("coef_t", [P, P])
        coef = sb("coef", [P, P])

        bank = [ctx.enter_context(nc.psum_tensor(f"bank{n}", [P, 512], F32)) for n in range(8)]

        ids_in = sem("ids_in")
        consts_in = sem("consts_in")
        consts_ready = sem("consts_ready")
        zeros_ready = sem("zeros_ready")
        bd_zeros_ready = sem("bd_zeros_ready")
        ids_ready = sem("ids_ready")
        gathered = [sem(f"gathered{p}") for p in range(2)]
        k_pair_in = [sem(f"k_pair_in{p}") for p in range(2)]
        q_bd_in = [sem(f"q_bd_in{p}") for p in range(2)]
        S = {n: sem(n) for n in (
            "idx_ready", "gv_ready", "gt_ready", "vt_ready", "gt_out", "vt_out", "ig_ready",
            "vi_ready",
            "cat_ready", "catv_ready", "fu_ready", "fused_ready", "ft_ready",
            "st1_ready", "mv1_ready", "rs1_ready", "rm1_ready", "t1_ready",
            "u0_ready", "u_ready", "h1_ready", "st2_ready", "mv2_ready", "rs2_ready", "x2_ready",
            "x2h_ready", "x2s_ready", "xt_ready", "x2t_ready", "q_ready", "k_ready", "v_ready",
            "qm_ready", "qs_ready", "kh_ready", "kl_ready", "v_lo_ready", "v_out", "k_bd_in",
            "s_ready", "max_ready", "mt_ready", "max_t_ready", "max_row_in", "st_ready",
            "prob_ready", "pv_ready", "rsum_ready", "o_ready", "ot_ready", "o_t_ready", "wo_ready",
            "h2_ready", "st3_ready", "mv3_ready", "rs3_ready", "x3_ready", "x3h_ready",
            "x3s_ready", "xw_ready", "w_ready", "r_ready", "x3t_ready", "x3t_out", "f1_ready",
            "hid_ready", "f2_ready", "y_ready",
        )}
        wT_ready, vector_step, coefT_ready, cT_ready, coef_ready = (
            sem(n) for n in ("wT_ready", "vector_step", "coefT_ready", "cT_ready", "coef_ready"))
        scaled, summed, pool_scaled, pool_summed = (
            sem(n) for n in ("scaled", "summed", "pool_scaled", "pool_summed"))
        act_scaled = sem("act_scaled")
        stored = sem("stored")
        passed = sem("passed")

        def wait(eng, name, per, g, k=None, alone=False):
            k = per if k is None else k
            if type(g) is int:
                if g < 0:
                    return
                if g >= NG:
                    g, k = NG - 1, per
            eng.wait_ge(S[name], g * per + k)
            if alone and type(g) is not int:
                eng.sem_inc(passed, 1)

        def ends(eng, name, per, g, k=None, alone=False):
            if type(g) is int:
                wait(eng, name, per, g, k, alone)

        def on(g):
            return type(g) is not int or 0 <= g < NG

        def of(tile, g):
            return tile[:, bass.ds(g * GB, GB)]

        def pipeline(eng, step, ahead=2):
            turns = (NG - ahead - FIRST) // 2
            for i in range(-2, FIRST):
                step(i, i % 2, i // 2)
            with eng.Fori(0, turns) as t:
                for odd in range(2):
                    step(t * 2 + (FIRST + odd), odd, t + FIRST // 2)
            for i in range(FIRST + 2 * turns, NG + 2):
                step(i, i % 2, i // 2)

        def late(i):
            return type(i) is int and i >= NG

        def ffn_bank(d, n):
            return bank[2 - n] if late(d + 1) else bank[7 - n]

        def wo_bank(e):
            return bank[3] if late(e + 1) else bank[6]

        block = ctx.enter_context(nc.Block())

        @block.sync
        def _(sp):
            sp.dma_start(ids_sb[:, :], ids).then_inc(ids_in, 16)
            sp.dma_start(wt[:, :], packed).then_inc(consts_in, 16)
            sp.wait_ge(zeros_ready, 4)
            sp.wait_ge(bd_zeros_ready, 1)

            def step(i, odd, half):
                b, c = i + 1, i
                if on(c):
                    wait(sp, "max_t_ready", 1, c)
                    wait(sp, "st_ready", GB, c - 1)
                    sp.dma_start(max_row[0:1, :, :].rearrange("p b (h q) -> p (b h) q", h=HEADS
                                                              ).bitcast(F32),
                                 max_t[:, :].bitcast(F32)).then_inc(S["max_row_in"], 16)
                if on(b):
                    wait(sp, "kh_ready", 1, b)
                    wait(sp, "s_ready", GB, b - 1)
                    for h in range(HEADS):
                        rows = slice(32 * h, 32 * h + 32)
                        sp.dma_start(k_bd[rows, :, h, :].bitcast(F32),
                                     k_hi[1 - odd][rows, :].rearrange("p (b k) -> p b k", b=GB
                                                                      ).bitcast(F32)
                                     ).then_inc(S["k_bd_in"], 16)
                    wait(sp, "st_ready", GB, b - 2)
                    for pair in range(2):
                        rows = slice(64 * pair, 64 * pair + 64)
                        sp.dma_start(k_pair[1 - odd][0:64, pair, :].bitcast(F32),
                                     k_hi[1 - odd][rows, :].bitcast(F32)
                                     ).then_inc(k_pair_in[1 - odd], 16)
                    wait(sp, "qs_ready", 1, b)
                    for h in range(HEADS):
                        rows = slice(32 * h, 32 * h + 32)
                        for part in range(2):
                            to = slice(64 * part + 32 * (h % 2), 64 * part + 32 * (h % 2) + 32)
                            sp.dma_start(q_bd[1 - odd][to, :, h // 2, h % 2, :].bitcast(F32),
                                         q_s[rows, :].rearrange("p (b q) -> p b q", b=GB
                                                                ).bitcast(F32)
                                         ).then_inc(q_bd_in[1 - odd], 16)
                    wait(sp, "kl_ready", 1, b)
                    for pair in range(2):
                        rows = slice(64 * pair, 64 * pair + 64)
                        sp.dma_start(k_pair[1 - odd][64:P, pair, :].bitcast(F32),
                                     k_lo[1 - odd][rows, :].bitcast(F32)
                                     ).then_inc(k_pair_in[1 - odd], 16)

            pipeline(sp, step)
            def store(first, count):
                sp.dma_start(out[first:first + count, :, :].rearrange("b t d -> t b d"),
                             R[:, first:first + count, :]).then_inc(stored, 16)

            n_dve = n_pool = 0
            for who in STORES:
                if who == "D":
                    sp.wait_ge(summed, n_dve + 1)
                    store(*DVE_SUMS[n_dve])
                    n_dve += 1
                else:
                    sp.wait_ge(pool_summed, n_pool + 1)
                    store(*POOL_SUMS[n_pool])
                    n_pool += 1
            sp.wait_ge(stored, 16 * len(STORES))

        @block.gpsimd
        def _(pool):
            def fetch(g, par):
                pool.tensor_copy(idx[par][:, :], of(idx_all, g)).then_inc(S["idx_ready"], 1)
                wait(pool, "idx_ready", 1, g, alone=True)
                wait(pool, "gt_ready", 1, g - 2, alone=True)
                wait(pool, "gv_ready", 1, g - 2, alone=True)
                wait(pool, "u_ready", 1, g - 2, alone=True)
                for b in range(GB):
                    pool.indirect_dma_start(
                        G[par][:, b, :], None, table,
                        bass.IndirectOffsetOnAxis(ap=idx[par][:, b:b + 1], axis=0),
                    ).then_inc(gathered[par], 16)

            def rstd(mv, rs, src, dst, g):
                wait(pool, src, 1, g, alone=True)
                pool.tensor_scalar(rs[:, :], mv[:, :, 1], LN_EPS, None, ALU.add
                                   ).then_inc(S[dst], 1)
                wait(pool, dst, 2, g, 1, alone=True)
                pool.tensor_tensor(rs[:, :], rs[:, :], minus_half[:, :], ALU.pow
                                   ).then_inc(S[dst], 1)

            def visit(g, par, g_half):
                pool.wait_ge(gathered[par], g_half * 64 + 64)
                wait(pool, "vt_ready", 1, g - 1, alone=True)
                pool.tensor_copy(gv[:, :, :], G[par][:, :, 2 * D:FEAT]).then_inc(S["gv_ready"], 1)

            pool.wait_ge(ids_ready, 2)
            fetch(0, 0)
            pool.memset(minus_half[:, :], -0.5)
            pool.memset(neg_max[:, :], 0.0)
            pool.memset(o[:, :, :], 0.0).then_inc(zeros_ready, 1)
            pool.wait_ge(zeros_ready, 1)
            pool.memset(o[:, :, D:D + 1], 1.0).then_inc(zeros_ready, 1)
            for p in range(2):
                last = pool.memset(V[p][:, :, :, HD:HD + 1], 1.0)
            last.then_inc(zeros_ready, 1)
            visit(0, 0, 0)
            pool.memset(max_row[:, :, :].bitcast(F32), 0.0).then_inc(zeros_ready, 1)
            pool.wait_ge(consts_ready, 1)

            def add_routed(n):
                first, count = POOL_SUMS[n]
                part = slice(first, first + count)
                pool.tensor_tensor(Y[:, part, :], Y[:, part, :],
                                   coef[:, part].unsqueeze(2).to_broadcast([P, count, D]),
                                   ALU.mult).then_inc(pool_scaled, 1)
                pool.wait_ge(pool_scaled, n + 1)
                pool.tensor_tensor(R[:, part, :], R[:, part, :], Y[:, part, :], ALU.add
                                   ).then_inc(pool_summed, 1)

            def step(i, odd, half):
                a, d, nxt = i + 2, i - 2, i + 3
                if on(d):
                    rstd(mv3, rs3, "mv3_ready", "rs3_ready", d)
                if on(nxt):
                    fetch(nxt, 1 - odd)
                if on(d):
                    wait(pool, "x3_ready", 1, d, alone=True)
                    wait(pool, "w_ready", 1, d - 1, alone=True)
                    pool.tensor_tensor(xw[:, :, :], x3[:, :, :],
                                       w["wr"].unsqueeze(1).to_broadcast([P, GB, D]), ALU.mult
                                       ).then_inc(S["xw_ready"], 1)
                    pool.tensor_tensor(of(R, d), of(R, d), x3[:, :, :], ALU.add
                                       ).then_inc(S["r_ready"], 1)
                if on(a):
                    wait(pool, "h1_ready", 1, a - 1, alone=True)
                    pool.tensor_tensor(
                        u0[:, :, :], of(valid, a).unsqueeze(2).to_broadcast([P, GB, D]),
                        b_tenth[:, :].unsqueeze(1).to_broadcast([P, GB, D]), ALU.mult
                    ).then_inc(S["u0_ready"], 1)
                    wait(pool, "u0_ready", 1, a, alone=True)
                    pool.tensor_tensor(u[:, :, :], u0[:, :, :], G[odd][:, :, 0:D], ALU.add
                                       ).then_inc(S["u_ready"], 1)
                if on(nxt):
                    visit(nxt, 1 - odd, half + 1 + odd)
                if on(a):
                    rstd(mv1, rs1, "mv1_ready", "rs1_ready", a)
                    wait(pool, "rs1_ready", 2, a, alone=True)
                    pool.tensor_tensor(rs1[:, :], rs1[:, :], of(valid, a), ALU.mult
                                       ).then_inc(S["rm1_ready"], 1)
                if on(a):
                    rstd(mv2, rs2, "mv2_ready", "rs2_ready", a)

                if type(i) is int and i >= NG - 1:
                    pool.wait_ge(coef_ready, 1)
                    wait(pool, "y_ready", 1, TAIL // GB - 1)
                    last = len(POOL_SUMS) - 1
                    for n in (range(2, last) if i > NG else (i - NG + 1,)):
                        add_routed(n)

            pipeline(pool, step, ahead=3)
            pool.wait_ge(coef_ready, 2)
            wait(pool, "y_ready", 1, NG - 2)
            add_routed(len(POOL_SUMS) - 1)

        @block.scalar
        def _(act):
            def scale_routed(n):
                act.wait_ge(coef_ready, 1)
                wait(act, "y_ready", 1, TAIL // GB - 1)
                first, count = DVE_SUMS[n]
                for q in range(first, first + count):
                    last = act.activation(Y[:, q, :], Y[:, q, :], ACT.Copy, scale=coef[:, q:q + 1])
                last.then_inc(act_scaled, 1)

            act.wait_ge(consts_ready, 1)
            act.wait_ge(zeros_ready, 3)

            def attention_out(e):
                wait(act, "ot_ready", 1, e)
                ends(act, "wo_ready", 1, e - 1)
                act.activation(o_t[:, :], bank[5][:, 0:GT // 2].bitcast(BF16), ACT.Copy
                               ).then_inc(S["o_t_ready"], 1)

            def step(i, odd, half):
                a, b, c, e, d = i + 2, i + 1, i, i - 1, i - 2
                if on(a):
                    wait(act, "gt_ready", 1, a)
                    act.activation(ig_in[:, :], bank[4][:, :], ACT.Copy).then_inc(S["gt_out"], 1)
                    wait(act, "vt_ready", 1, a)
                    act.activation(vi_in[0:GB * VD, :], bank[5][0:GB * VD, 0:P], ACT.Copy
                                   ).then_inc(S["vt_out"], 1)
                    wait(act, "ig_ready", 1, a)
                    act.activation(cat[:, :], bank[6][:, :], ACT.Gelu, bias=w["b_ig"]
                                   ).then_inc(S["cat_ready"], 1)
                    wait(act, "vi_ready", 1, a)
                    act.activation(catv[:, :], bank[7][:, 0:2 * P], ACT.Gelu, bias=w["b_vi"]
                                   ).then_inc(S["catv_ready"], 1)
                if on(a):
                    wait(act, "fu_ready", 1, a)
                    ends(act, "ft_ready", 1, a - 1)
                    act.activation(fused[:, :], bank[6][:, 0:2 * P], ACT.Gelu, bias=w["b_fu"]
                                   ).then_inc(S["fused_ready"], 1)
                if on(b):
                    wait(act, "xt_ready", 1, b)
                    ends(act, "v_ready", 1, b - 1)
                    act.activation(x2t[:, :], bank[4][:, :], ACT.Copy).then_inc(S["x2t_ready"], 1)
                if on(c):
                    wait(act, "mt_ready", 1, c)
                    ends(act, "max_row_in", 16, c - 1)
                    act.activation(max_t[:, :], bank[0][0:GB * HEADS, 0:P], ACT.Copy
                                   ).then_inc(S["max_t_ready"], 1)
                if on(b):
                    wait(act, "q_ready", 1, b)
                    ends(act, "qs_ready", 1, b - 1)
                    act.activation(q_mask[:, :].bitcast(F32R), bank[4][:, :], ACT.Identity,
                                   bias=bq_lo[:, :], scale=w["lo_row"]).then_inc(S["qm_ready"], 1)
                if late(i):
                    scale_routed(ACT_SCALES[i - NG])
                if on(d):
                    wait(act, "x3t_ready", 1, d)
                    act.activation(x3t[:, :], ffn_bank(d, 0)[:, :], ACT.Copy
                                   ).then_inc(S["x3t_out"], 1)
                if on(e) and late(i):
                    attention_out(e)
                if on(b):
                    wait(act, "k_ready", 1, b)
                    if on(b - 2):
                        act.wait_ge(k_pair_in[1 - odd], (half + odd) * 64)
                    ends(act, "k_bd_in", 64, b - 2)
                    act.activation(k_hi[1 - odd][:, :], bank[3][:, :], ACT.Identity,
                                   bias=w["b_k"]).then_inc(S["kh_ready"], 1)
                if on(d):
                    ends(act, "f2_ready", 1, d - 1)
                    for m in range(2):
                        wait(act, "f1_ready", 2, d, m + 1)
                        act.activation(hid[:, m, :], ffn_bank(d, m)[:, :], ACT.Gelu_apprx_tanh,
                                       bias=w["b_1"][:, m:m + 1]).then_inc(S["hid_ready"], 1)
                for s in range(GB):
                    if on(c):
                        ends(act, "pv_ready", 1, c - 1)
                        wait(act, "st_ready", GB, c, s + 1)
                        act.activation(prob[:, s, :, :].rearrange("p h q -> p (h q)"),
                                       bank[s][:, :], ACT.Exp, scale=SCALE
                                       ).then_inc(S["prob_ready"], 1)
                    if s == 0 and on(e) and not late(i):
                        attention_out(e)

            pipeline(act, step)

        @block.vector
        def _(dve):
            dve.wait_ge(ids_in, 16)
            dve.tensor_scalar(idx_all[:, :], ids_sb[:, :], 0, 25000, ALU.max, ALU.min
                              ).then_inc(ids_ready, 1)
            dve.tensor_scalar(valid[:, :], ids_sb[:, :], 0, None, ALU.not_equal
                              ).then_inc(ids_ready, 1)
            dve.memset(ones_r[:, :].bitcast(F32), 1.0)
            dve.wait_ge(consts_in, 16)
            dve.tensor_copy(w_hi[:, :], wt[:, 0:SPLIT])
            dve.tensor_copy(v_parts[:, 0, :], w["w_v"])
            dve.tensor_copy(wo_part[:, 0, :], w["w_o"])
            dve.tensor_copy(ident_bf[:, :], ident)
            dve.tensor_scalar(g_tenth[:, :], w["gamma"], 0.1, None, ALU.mult)
            dve.tensor_scalar(b_tenth[:, :], w["beta"], 0.1, None, ALU.mult)
            dve.tensor_tensor(bq_lo[:, :], w["b_q"], w["lo_row"], ALU.mult).then_inc(vector_step, 1)
            dve.wait_ge(vector_step, 1)
            dve.tensor_tensor(w_lo[:, :], wt[:, 0:SPLIT], w_hi[:, :].bitcast(F32), ALU.subtract)
            dve.tensor_tensor(v_parts[:, 1, :], w["w_v"], v_parts[:, 0, :].bitcast(F32),
                              ALU.subtract)
            dve.tensor_tensor(wo_rest[:, 0, :], w["w_o"], wo_part[:, 0, :], ALU.subtract
                              ).then_inc(vector_step, 1)
            dve.wait_ge(vector_step, 2)
            dve.tensor_copy(wo_part[:, 1, :], wo_rest[:, 0, :]).then_inc(vector_step, 1)
            dve.wait_ge(vector_step, 3)
            dve.tensor_tensor(wo_rest[:, 1, :], wo_rest[:, 0, :], wo_part[:, 1, :], ALU.subtract
                              ).then_inc(vector_step, 1)
            dve.wait_ge(vector_step, 4)
            dve.tensor_copy(wo_part[:, 2, :], wo_rest[:, 1, :]).then_inc(consts_ready, 1)
            for tile in q_bd:
                dve.memset(tile[:, :, :, :, :].bitcast(F32), 0.0)
            dve.memset(k_bd[:, :, :, :].bitcast(F32), 0.0).then_inc(bd_zeros_ready, 1)
            setup_steps = 4
            dve.wait_ge(consts_ready, 1)
            dve.wait_ge(zeros_ready, 3)

            def stats(src, st, done, g):
                for b in range(GB):
                    last = dve.bn_stats(st[:, b, :], src(b))
                last.then_inc(S[done], 1)

            def moments(st, mv, st_done, mv_done, g):
                wait(dve, st_done, 1, g, alone=True)
                for b in range(GB):
                    last = dve.bn_aggr(mv[:, b, :], st[:, b, :])
                last.then_inc(S[mv_done], 1)

            def normalize(dst, src, mv, rs, done, g):
                for b in range(GB):
                    last = dve.tensor_scalar(dst[:, b, :], src(b), mv[:, b, 0:1], rs[:, b:b + 1],
                                             ALU.subtract, ALU.mult)
                last.then_inc(S[done], 1)

            def split_hi(dst, src, done):
                dve.tensor_copy(dst[:, :, 0, :], src[:, :, :]).then_inc(S[done], 1)

            def split_lo(dst, src, hi_done, done, g):
                wait(dve, hi_done, 1, g)
                dve.tensor_tensor(dst[:, :, 1, :], src[:, :, :], dst[:, :, 0, :].bitcast(F32),
                                  ALU.subtract).then_inc(S[done], 1)

            def kept(g):
                return lambda s: R[:, bass.ds(g * GB + s, 1), :].rearrange("p b d -> p (b d)")

            ft = bank[5][:, 0:GB * D].rearrange("p (b d) -> p b d", b=GB)

            n = [setup_steps]

            def done(ins):
                n[0] += 1
                ins.then_inc(vector_step, 1)
                dve.wait_ge(vector_step, n[0])

            def take_weights(part):
                rows = slice(0, PARTS[part][1] - PARTS[part][0])
                dve.wait_ge(wT_ready, part + 1)
                done(dve.tensor_scalar(wt_rank[rows, :], bank[4 * (1 - part)][rows, 0:P],
                                       w["br"][rows, :], None, ALU.add))

            def rounds(part, r0, r1):
                rows = slice(0, PARTS[part][1] - PARTS[part][0])
                for r in range(r0, r1):
                    src = left if r else wt_rank
                    done(dve.max(top[rows, :], src[rows, :]))
                    done(dve.match_replace(left[rows, :], top[rows, :], src[rows, :], LOWEST))

            def select(part):
                rows = slice(0, PARTS[part][1] - PARTS[part][0])
                done(dve.max(top[rows, :], left[rows, :]))
                least = top[rows, KEEP % 8 - 1:KEEP % 8]
                dve.tensor_scalar(over[rows, :], wt_rank[rows, :], least, None, ALU.is_gt)
                done(dve.tensor_scalar(equal[rows, :], wt_rank[rows, :], least, None,
                                       ALU.is_equal))
                dve.tensor_reduce(room[rows, :], over[rows, :], AX, ALU.add, negate=True)
                done(dve.tensor_tensor_scan(order[rows, :], ones_r[rows, :].bitcast(F32),
                                            equal[rows, :], 0.0, ALU.mult, ALU.add))
                done(dve.tensor_scalar(room[rows, :], room[rows, :], float(KEEP), None, ALU.add))
                done(dve.scalar_tensor_tensor(order[rows, :], order[rows, :], room[rows, :],
                                              equal[rows, :], ALU.is_le, ALU.mult))
                done(dve.tensor_tensor(order[rows, :], order[rows, :], over[rows, :], ALU.add))
                dve.tensor_tensor(coef_t[rows, :], order[rows, :], wt_rank[rows, :], ALU.mult
                                  ).then_inc(coefT_ready, 1)

            def take_coef(part):
                dve.wait_ge(cT_ready, part + 1)
                first, end = PARTS[part]
                dve.tensor_copy(coef[:, first:end], bank[4][:, 0:end - first]
                                ).then_inc(coef_ready, 1)
                dve.wait_ge(coef_ready, part + 1)

            def add_routed(n):
                first, count = DVE_SUMS[n]
                part = slice(first, first + count)
                if n in ACT_SCALES:
                    dve.wait_ge(act_scaled, ACT_SCALES.index(n) + 1)
                else:
                    dve.tensor_tensor(Y[:, part, :], Y[:, part, :],
                                      coef[:, part].unsqueeze(2).to_broadcast([P, count, D]),
                                      ALU.mult).then_inc(scaled, 1)
                    dve.wait_ge(scaled, n + 1 - sum(m < n for m in ACT_SCALES))
                dve.tensor_tensor(R[:, part, :], R[:, part, :], Y[:, part, :], ALU.add
                                  ).then_inc(summed, 1)

            def ffn_out(d):
                wait(dve, "f2_ready", 1, d)
                dve.tensor_tensor(
                    of(Y, d), ffn_bank(d, 0)[:, 0:GB * D].rearrange("p (b d) -> p b d", b=GB),
                    w["b2"].unsqueeze(1).to_broadcast([P, GB, D]), ALU.add
                ).then_inc(S["y_ready"], 1)

            def maxima(c, seqs):
                for s in seqs:
                    wait(dve, "s_ready", GB, c, s + 1)
                    dve.tensor_reduce(neg_max[:, HEADS * s:HEADS * s + HEADS],
                                      bank[s][:, :].rearrange("p (h k) -> p h k", h=HEADS),
                                      AX, ALU.max, negate=True).then_inc(S["max_ready"], 1)

            def step(i, odd, half):
                a, b, c, e, d = i + 2, i + 1, i, i - 1, i - 2
                if on(d):
                    wait(dve, "wo_ready", 1, d)
                    dve.tensor_tensor(of(R, d), of(R, d),
                                      wo_bank(d)[:, 0:GB * D].rearrange("p (b d) -> p b d", b=GB),
                                      ALU.add).then_inc(S["h2_ready"], 1)
                if on(b):
                    moments(st2, mv2, "st2_ready", "mv2_ready", b)
                if on(d):
                    wait(dve, "h2_ready", 1, d, alone=True)
                    stats(kept(d), st3, "st3_ready", d)
                if on(c):
                    maxima(c, (0,))
                if on(d):
                    moments(st3, mv3, "st3_ready", "mv3_ready", d)
                if on(c):
                    maxima(c, (1,))
                if type(i) is int and i == NG - 2:
                    take_weights(0)
                if on(b):
                    wait(dve, "rs2_ready", 2, b)
                    normalize(x2, kept(b), mv2, rs2, "x2_ready", b)
                    wait(dve, "x2_ready", 1, b)
                    ends(dve, "xt_ready", 1, b - 1)
                    split_hi(x2s, x2, "x2h_ready")
                    split_lo(x2s, x2, "x2h_ready", "x2s_ready", b)
                if on(c):
                    maxima(c, (2, 3))
                if late(i):
                    add_routed(1 if i == NG else 4)
                if on(d):
                    wait(dve, "rs3_ready", 2, d)
                    ends(dve, "r_ready", 1, d - 1)
                    normalize(x3, kept(d), mv3, rs3, "x3_ready", d)
                    wait(dve, "x3_ready", 1, d)
                    ends(dve, "x3t_ready", 1, d - 1)
                    split_hi(x3s, x3, "x3h_ready")
                    split_lo(x3s, x3, "x3h_ready", "x3s_ready", d)
                if on(e):
                    pv = bank[5][:, 0:GB * HEADS * (HD + 1)].rearrange(
                        "p (b h d) -> p b h d", b=GB, h=HEADS)
                    wait(dve, "pv_ready", 1, e)
                    dve.reciprocal(rsum[:, :, :], pv[:, :, :, HD]).then_inc(S["rsum_ready"], 1)
                    wait(dve, "rsum_ready", 1, e)
                    ends(dve, "ot_ready", 1, e - 1)
                    dve.tensor_tensor(
                        o[:, :, 0:D].rearrange("p b (h d) -> p b h d", h=HEADS), pv[:, :, :, 0:HD],
                        rsum[:, :, :].unsqueeze(3).to_broadcast([P, GB, HEADS, HD]), ALU.mult
                    ).then_inc(S["o_ready"], 1)
                if on(b):
                    wait(dve, "qm_ready", 1, b)
                    if on(c):
                        dve.wait_ge(q_bd_in[odd], half * 128 + 128)
                    ends(dve, "s_ready", GB, b - 1)
                    dve.scalar_tensor_tensor(q_s[:, :], bank[4][:, :], w["b_q"], q_mask[:, :],
                                             ALU.add, ALU.subtract).then_inc(S["qs_ready"], 1)
                if on(a):
                    wait(dve, "ft_ready", 1, a, alone=True)
                    stats(lambda s: ft[:, s, :], st1, "st1_ready", a)
                if on(b):
                    wait(dve, "kh_ready", 1, b)
                    if on(b - 2):
                        dve.wait_ge(k_pair_in[1 - odd], (half + odd) * 64)
                    dve.scalar_tensor_tensor(k_lo[1 - odd][:, :], bank[3][:, :], w["b_k"],
                                             k_hi[1 - odd][:, :].bitcast(F32),
                                             ALU.add, ALU.subtract).then_inc(S["kl_ready"], 1)
                if on(a):
                    moments(st1, mv1, "st1_ready", "mv1_ready", a)
                    wait(dve, "mv1_ready", 1, a)
                    for s in range(GB):
                        last = dve.scalar_tensor_tensor(t1[:, s, :], ft[:, s, :], mv1[:, s, 0:1],
                                                        g_tenth[:, :], ALU.subtract, ALU.mult)
                    last.then_inc(S["t1_ready"], 1)
                if on(b):
                    wait(dve, "v_ready", 1, b)
                    ends(dve, "pv_ready", 1, b - 2)
                    v_new = V[1 - odd][:, :, :, 0:HD]
                    v_ps = bank[4][:, :].rearrange("p (b k h d) -> p b k h d", b=GB, k=2, h=HEADS)
                    dve.tensor_tensor(
                        v_new, v_ps[:, :, 1],
                        w["bv"].rearrange("p (h d) -> p h d", h=HEADS).unsqueeze(1).to_broadcast(
                            [P, GB, HEADS, HD]), ALU.add).then_inc(S["v_lo_ready"], 1)
                if on(d):
                    wait(dve, "xw_ready", 1, d)
                    dve.tensor_reduce(of(W, d), xw[:, :, :], AX, ALU.add
                                      ).then_inc(S["w_ready"], 1)
                if on(b):
                    wait(dve, "v_lo_ready", 1, b)
                    dve.tensor_tensor(v_new, v_new, v_ps[:, :, 0], ALU.add
                                      ).then_inc(S["v_out"], 1)
                if on(a):
                    ends(dve, "t1_ready", 1, a)
                    ends(dve, "u_ready", 1, a)
                    wait(dve, "rm1_ready", 1, a)
                    for s in range(GB):
                        last = dve.scalar_tensor_tensor(kept(a)(s), t1[:, s, :], rs1[:, s:s + 1],
                                                        u[:, s, :], ALU.mult, ALU.add)
                    last.then_inc(S["h1_ready"], 1)
                if on(a):
                    wait(dve, "h1_ready", 1, a, alone=True)
                    stats(kept(a), st2, "st2_ready", a)
                if type(i) is int and i == NG - 2:
                    rounds(0, 0, SPLIT_ROUNDS)
                if type(i) is int and i == NG - 1:
                    rounds(0, SPLIT_ROUNDS, KEEP // 8)
                    select(0)
                if type(i) is int and i == NG - 1:
                    take_coef(0)
                    wait(dve, "r_ready", 1, TAIL // GB - 1)
                    add_routed(0)
                if on(d) and not late(i):
                    ffn_out(d)
                if type(i) is int and i == NG:
                    add_routed(2)
                    add_routed(3)

            pipeline(dve, step)

            take_weights(1)
            rounds(1, 0, KEEP // 8)
            select(1)
            ffn_out(NG - 2)
            add_routed(5)
            take_coef(1)
            wait(dve, "r_ready", 1, NG - 1)
            add_routed(6)
            ffn_out(NG - 1)
            wait(dve, "y_ready", 1, NG - 1)
            add_routed(7)

        @block.tensor
        def _(pe):
            pe.wait_ge(consts_ready, 1)
            pe.wait_ge(zeros_ready, 3)
            mm = nc.tensor.matmul

            def attention_t(e):
                ends(pe, "o_ready", 1, e)
                wait(pe, "t1_ready", 1, e + 3)
                for s in range(GB):
                    last = mm(bank[5][:, s * P // 2:(s + 1) * P // 2].bitcast(BF16),
                              o[:, s, :], ident_bf[:, :], start=True, stop=True,
                              is_transpose=True)
                last.then_inc(S["ot_ready"], 1)

            def project(e):
                wait(pe, "o_t_ready", 1, e)
                if late(e + 1):
                    ends(pe, "prob_ready", GB, e)
                else:
                    ends(pe, "hid_ready", 2, e - 1)
                for s in range(GB):
                    for n in range(3):
                        last = mm(wo_bank(e)[:, s * D:(s + 1) * D],
                                  o_t[0:D + 1, s * P:(s + 1) * P], wo_part[0:D + 1, n, :],
                                  start=(n == 0), stop=(n == 2))
                last.then_inc(S["wo_ready"], 1)

            def ffn_second(d):
                wait(pe, "hid_ready", 2, d)
                for s in range(GB):
                    for m in range(2):
                        last = mm(ffn_bank(d, 0)[:, s * D:(s + 1) * D],
                                  hid[:, m, s * P:(s + 1) * P], w["w_2"][:, m * D:(m + 1) * D],
                                  start=(m == 0), stop=(m == 1))
                last.then_inc(S["f2_ready"], 1)

            def weights_t(part):
                first, end = PARTS[part]
                wait(pe, "w_ready", 1, end // GB - 1)
                wait(pe, "v_out", 1, NG - 2 + part)
                mm(bank[4 * (1 - part)][0:end - first, 0:P], W[:, first:end], ident,
                   start=True, stop=True, is_transpose=True).then_inc(wT_ready, 1)

            def coefficients(part):
                rows = slice(0, PARTS[part][1] - PARTS[part][0])
                pe.wait_ge(coefT_ready, part + 1)
                mm(bank[4][:, rows], coef_t[rows, :], ident[rows, rows],
                   start=True, stop=True, is_transpose=True).then_inc(cT_ready, 1)

            def values(e, odd, seqs):
                for s in seqs:
                    for h in range(HEADS):
                        at = (s * HEADS + h) * (HD + 1)
                        last = mm(bank[5][:, at:at + HD + 1], prob[:, s, h, :],
                                  V[1 - odd][:, s, h, :], start=True, stop=True)
                return last

            def scores_t(c, odd, seqs):
                for s in seqs:
                    tok = slice(s * P, (s + 1) * P)
                    mm(bank[s][:, :], ones_r[:, :], max_row[:, s, :], start=True, stop=False)
                    for pair in range(2):
                        last = mm(bank[s][:, pair * 2 * P:(pair + 1) * 2 * P],
                                  k_pair[odd][:, pair, tok],
                                  q_bd[odd][:, s, pair, :, :].rearrange("p h q -> p (h q)"),
                                  start=False, stop=(pair == 1))
                    last.then_inc(S["st_ready"], 1)

            def step(i, odd, half):
                a, b, c, e, d = i + 2, i + 1, i, i - 1, i - 2
                if type(i) is int and i == NG - 2:
                    weights_t(0)
                if type(i) is int and i == NG + 1:
                    weights_t(1)
                if on(a):
                    pe.wait_ge(gathered[odd], (half + 1) * 64 + 64)
                    wait(pe, "v_out", 1, a - 2)
                    for s in range(GB):
                        last = mm(bank[4][:, s * P:(s + 1) * P], G[odd][:, s, 0:2 * D], ident,
                                  start=True, stop=True, is_transpose=True)
                    last.then_inc(S["gt_ready"], 1)
                if on(a):
                    wait(pe, "gv_ready", 1, a)
                    ends(pe, "t1_ready", 1, a - 1)
                    wait(pe, "o_t_ready", 1, a - 4)
                    mm(bank[5][0:GB * VD, 0:P], gv[:, :, :].rearrange("p b d -> p (b d)"), ident,
                       start=True, stop=True, is_transpose=True).then_inc(S["vt_ready"], 1)
                if on(c):
                    wait(pe, "k_bd_in", 64, c)
                    ends(pe, "qs_ready", 1, c)
                    for s in range(GB):
                        wait(pe, "prob_ready", GB, c - 1, s + 1)
                        mm(bank[s][:, :], q_s[:, s * P:(s + 1) * P],
                           k_bd[:, s, :, :].rearrange("p h k -> p (h k)"), start=True, stop=True
                           ).then_inc(S["s_ready"], 1)
                if on(a):
                    wait(pe, "gt_out", 1, a)
                    wait(pe, "h2_ready", 1, a - 4)
                    mm(bank[6][:, :], w["w_ig"], ig_in[:, :], start=True, stop=True
                       ).then_inc(S["ig_ready"], 1)
                if on(e):
                    ends(pe, "prob_ready", GB, e)
                    ends(pe, "v_out", 1, e)
                    wait(pe, "vt_out", 1, e + 3)
                    values(e, odd, (0,))
                if on(a):
                    wait(pe, "vt_out", 1, a)
                    ends(pe, "y_ready", 1, a - 5)
                    for n in range(2):
                        last = mm(bank[7][:, n * P:(n + 1) * P],
                                  w["w_vi"][0:GB * VD, n * P:(n + 1) * P], vi_in[0:GB * VD, :],
                                  start=True, stop=True)
                    last.then_inc(S["vi_ready"], 1)
                if on(e):
                    values(e, odd, (1,))
                if on(a):
                    wait(pe, "catv_ready", 1, a)
                    mm(bank[6][:, 0:2 * P], w["w_fv"], catv[:, :], start=True, stop=False)
                    for n, wf in enumerate(("w_fe", "w_fo")):
                        last = mm(bank[6][:, 0:2 * P], w[wf],
                                  cat[:, :].rearrange("p (r s q) -> p s r q", r=2, s=2)[:, n],
                                  start=False, stop=(n == 1))
                    last.then_inc(S["fu_ready"], 1)
                if on(b):
                    wait(pe, "x2s_ready", 1, b)
                    ends(pe, "gt_out", 1, b + 1)
                    for s in range(GB):
                        last = mm(bank[4][:, s * P:(s + 1) * P],
                                  x2s[:, s, :, :].rearrange("p k d -> p (k d)").bitcast(F32),
                                  ident, start=True, stop=True, is_transpose=True)
                    last.then_inc(S["xt_ready"], 1)
                if on(e):
                    values(e, odd, (2,))
                if on(c):
                    wait(pe, "max_ready", GB, c)
                    mm(bank[0][:, 0:P], neg_max[:, :], ident, start=True, stop=True,
                       is_transpose=True).then_inc(S["mt_ready"], 1)
                if on(b):
                    wait(pe, "x2t_ready", 1, b)
                    mm(bank[4][:, :], hi["w_q"], x2t[:, :], start=True, stop=False)
                    mm(bank[4][:, :], lo["w_q"], x2t[:, :], start=False, stop=True
                       ).then_inc(S["q_ready"], 1)
                if on(e):
                    values(e, odd, (3,)).then_inc(S["pv_ready"], 1)
                if on(d):
                    wait(pe, "x3s_ready", 1, d)
                    ends(pe, "catv_ready", 1, d + 4)
                    for s in range(GB):
                        last = mm(ffn_bank(d, 0)[:, s * P:(s + 1) * P],
                                  x3s[:, s, :, :].rearrange("p k d -> p (k d)").bitcast(F32),
                                  ident, start=True, stop=True, is_transpose=True)
                    last.then_inc(S["x3t_ready"], 1)
                if on(b):
                    ends(pe, "max_ready", GB, b - 1)
                    mm(bank[3][:, :], hi["w_k"], x2t[:, :], start=True, stop=False)
                    mm(bank[3][:, :], lo["w_k"], x2t[:, :], start=False, stop=True
                       ).then_inc(S["k_ready"], 1)
                if on(e) and late(i):
                    attention_t(e)
                    project(e)
                if type(i) is int and i == NG + 1:
                    ffn_second(NG - 2)
                if on(a):
                    wait(pe, "fused_ready", 1, a)
                    wait(pe, "o_ready", 1, a - 3)
                    for n in range(2):
                        last = mm(bank[5][:, n * P:(n + 1) * P], fused[:, n * P:(n + 1) * P],
                                  ident, start=True, stop=True, is_transpose=True)
                    last.then_inc(S["ft_ready"], 1)
                if on(d):
                    wait(pe, "x3t_out", 1, d)
                    ends(pe, "fused_ready", 1, d + 4)
                    for m in range(2):
                        cols = slice(m * P, (m + 1) * P)
                        mm(ffn_bank(d, m)[:, :], hi["w_1"][:, cols], x3t[:, :],
                           start=True, stop=False)
                        mm(ffn_bank(d, m)[:, :], lo["w_1"][:, cols], x3t[:, :],
                           start=False, stop=True
                           ).then_inc(S["f1_ready"], 1)
                if on(b):
                    wait(pe, "qs_ready", 1, b)
                    for s in range(GB):
                        last = mm(bank[4][:, s * P:(s + 1) * P], x2t[:, s * P:(s + 1) * P],
                                  v_parts[:, :, :].rearrange("p k d -> p (k d)"),
                                  start=True, stop=True)
                    last.then_inc(S["v_ready"], 1)
                if on(c):
                    wait(pe, "max_row_in", 16, c)
                    pe.wait_ge(q_bd_in[odd], half * 128 + 128)
                    pe.wait_ge(k_pair_in[odd], half * 64 + 64)
                    scores_t(c, odd, (0,))
                if on(c):
                    scores_t(c, odd, (1, 2))
                    if type(c) is int and c == NG - 1:
                        coefficients(0)
                    wait(pe, "kl_ready", 1, c + 1)
                    scores_t(c, odd, (3,))
                if on(e) and not late(i):
                    attention_t(e)
                if on(d) and not late(i):
                    ffn_second(d)
                if on(e) and not late(i):
                    project(e)

            pipeline(pe, step)
            coefficients(1)
            ffn_second(NG - 1)


def kernel(x, L0_tok_emb_table, L0_tok_geo_table, L0_tok_visit_table, L0_tok_w_item,
           L0_tok_b_item, L0_tok_w_geo, L0_tok_b_geo, L0_tok_w_visit, L0_tok_b_visit,
           L0_tok_w_fuse, L0_tok_b_fuse, L0_tok_ln_gamma, L0_tok_ln_beta, L0_attn_Wq, L0_attn_bq,
           L0_attn_Wk, L0_attn_bk, L0_attn_Wv, L0_attn_bv, L0_attn_Wo, L0_attn_bo,
           L0_ffn_attention_mask, L0_ffn_wr, L0_ffn_br, L0_ffn_w1, L0_ffn_b1, L0_ffn_w2,
           L0_ffn_b2):
    import numpy as np
    import concourse.bacc as bacc
    from concourse.bass_utils import run_bass_kernel_spmd

    c = {n: np.zeros((P, b - a), np.float32) for n, (a, b) in COL.items()}

    def per_head(wt):
        wt = wt.reshape(wt.shape[0], HEADS, 1, HD)
        return np.broadcast_to(wt, (wt.shape[0], HEADS, 2, HD)).reshape(wt.shape[0], P)

    for n, src in (("w_q", L0_attn_Wq), ("w_k", L0_attn_Wk)):
        c[n][:D] = c[n][D:] = per_head(np.asarray(src).T)
    c["w_v"][:D] = c["w_v"][D:] = np.asarray(L0_attn_Wv).T
    c["w_1"][:D] = c["w_1"][D:] = np.asarray(L0_ffn_w1)
    c["w_ig"][:D, :D] = np.asarray(L0_tok_w_item)
    c["w_ig"][D:, D:] = np.asarray(L0_tok_w_geo)
    for s in range(GB):
        at = (s // 2) * P + (s % 2) * D
        c["w_vi"][s * VD:(s + 1) * VD, at:at + D] = np.asarray(L0_tok_w_visit)
    wf = np.asarray(L0_tok_w_fuse)
    c["w_fe"][:, :D] = c["w_fo"][:, D:] = wf[:P]
    c["w_fv"][:D, :D] = c["w_fv"][D:, D:] = wf[P:]
    c["w_2"][:, :D], c["w_2"][:, D:] = np.asarray(L0_ffn_w2)[:P], np.asarray(L0_ffn_w2)[P:]
    c["w_o"][:D], c["w_o"][D] = np.asarray(L0_attn_Wo).T, np.asarray(L0_attn_bo)
    c["ident"][:] = np.eye(P, dtype=np.float32)
    for n, src in (("gamma", L0_tok_ln_gamma), ("beta", L0_tok_ln_beta), ("bv", L0_attn_bv),
                   ("b2", L0_ffn_b2), ("wr", L0_ffn_wr), ("br", L0_ffn_br)):
        c[n][:] = np.asarray(src).reshape(1, -1)
    c["b_ig"][:D, 0], c["b_ig"][D:, 0] = np.asarray(L0_tok_b_item), np.asarray(L0_tok_b_geo)
    for n, src in (("b_vi", L0_tok_b_visit), ("b_fu", L0_tok_b_fuse)):
        c[n][:D, 0] = c[n][D:, 0] = np.asarray(src)
    for n, src in (("b_q", L0_attn_bq), ("b_k", L0_attn_bk)):
        c[n][:, 0] = per_head(np.asarray(src).reshape(1, D))[0]
    c["b_1"][:, 0], c["b_1"][:, 1] = np.asarray(L0_ffn_b1)[:P], np.asarray(L0_ffn_b1)[P:]
    c["lo_row"][:, 0] = np.arange(P) // HD % 2

    arrays = {
        "ids": np.ascontiguousarray(np.asarray(x).T),
        "table": np.concatenate([np.asarray(L0_tok_emb_table), np.asarray(L0_tok_geo_table),
                                 np.asarray(L0_tok_visit_table)], axis=1),
        "packed": np.concatenate([c[n] for n, _ in _COLS], axis=1),
    }
    nc = bacc.Bacc("TRN2", target_bir_lowering=False, num_devices=1)
    args = [nc.dram_tensor(n, a.shape, mybir.dt.from_np(a.dtype), kind="ExternalInput").ap()
            for n, a in arrays.items()]
    out = nc.dram_tensor("out", (P, P, D), F32, kind="ExternalOutput").ap()
    build(nc, *args, out)
    r = run_bass_kernel_spmd(nc, [arrays], core_ids=[0])
    return r.results[0]["out"]
```
